# Optimizing a Trainium2 kernel written in Bass

```python
import numpy as np
import jax
import jax.numpy as jnp

def _softmax(x, axis=-1):
    return jax.nn.softmax(x, axis=axis)

def _gelu(x):
    return jax.nn.gelu(x, approximate=True)

def _silu(x):
    return jax.nn.silu(x)

def _sigmoid(x):
    return jax.nn.sigmoid(x)

def _layernorm(x, axis=-1, eps=1e-05):
    m = jnp.mean(x, axis=axis, keepdims=True)
    v = jnp.var(x, axis=axis, keepdims=True)
    return (x - m) / jnp.sqrt(v + eps)

def _scatter_add(tgt, idx, src, axis=0):
    return tgt.at[idx].add(src)

def _segment_sum(src, seg, n):
    return jax.ops.segment_sum(src, seg, n)
kernel_name = 'mk_seq_postln_d1_jaxref_r4_234f24'

def setup_inputs(seed: int=0):
    np.random.seed(seed)
    _w = jnp.asarray

    def _L0_attn_setup():
        import jax, jax.numpy as jnp
        import numpy as np
        D_MODEL = 256
        NUM_HEADS = 4
        KEY_DIM = 256
        VALUE_DIM = 512
        HEAD_QK = KEY_DIM // NUM_HEADS
        HEAD_V = VALUE_DIM // NUM_HEADS
        EPS = 1e-05
        CHUNK = 64
        ROPE_BASE = 10000.0

        def apply_rotary(q, k):
            n, d = (q.shape[1], q.shape[-1])
            inv_freq = 1.0 / ROPE_BASE ** (jnp.arange(0, d, 2, dtype=jnp.float32) / d)
            t = jnp.arange(n, dtype=jnp.float32)
            freqs = jnp.outer(t, inv_freq)
            cos = jnp.cos(freqs)[None, :, None, :]
            sin = jnp.sin(freqs)[None, :, None, :]

            def rot(x):
                x1, x2 = jnp.split(x, 2, axis=-1)
                return jnp.concatenate([x1 * cos - x2 * sin, x2 * cos + x1 * sin], axis=-1)
            return (rot(q), rot(k))

        def chunk_retention(q, k, v, gamma, chunk=CHUNK):
            B, H, N, dk = q.shape
            dv = v.shape[-1]
            NC = N // chunk
            qc = jnp.moveaxis(q.reshape(B, H, NC, chunk, dk), 2, 0)
            kc = jnp.moveaxis(k.reshape(B, H, NC, chunk, dk), 2, 0)
            vc = jnp.moveaxis(v.reshape(B, H, NC, chunk, dv), 2, 0)
            idx = jnp.arange(chunk)
            rel = idx[:, None] - idx[None, :]
            D = jnp.where(rel >= 0, gamma[:, None, None] ** rel, 0.0)
            cross_q = (gamma[:, None] ** (idx + 1))[None, :, :, None]
            cross_k = (gamma[:, None] ** (chunk - 1 - idx))[None, :, :, None]
            gC = (gamma ** chunk)[None, :, None, None]

            def step(S, qkv):
                qb, kb, vb = qkv
                attn = jnp.einsum('bhid,bhjd->bhij', qb, kb) * D[None]
                o_intra = jnp.einsum('bhij,bhjd->bhid', attn, vb)
                o_inter = jnp.einsum('bhid,bhde->bhie', qb * cross_q, S)
                S_new = gC * S + jnp.einsum('bhjd,bhje->bhde', kb * cross_k, vb)
                return (S_new, o_intra + o_inter)
            S0 = jnp.zeros((B, H, dk, dv), dtype=q.dtype)
            _, o = jax.lax.scan(step, S0, (qc, kc, vc))
            return jnp.moveaxis(o, 0, 2).reshape(B, H, N, dv)

        def rmsnorm(x, w):
            var = jnp.mean(x * x, axis=-1, keepdims=True)
            return x * jax.lax.rsqrt(var + EPS) * w
        key = jax.random.key(seed)
        ks = jax.random.split(key, 7)
        B, N = (2, 1024)
        s = 0.02
        return {'x': jax.random.normal(ks[0], (B, N, D_MODEL), dtype=jnp.float32), 'Wq': jax.random.normal(ks[1], (D_MODEL, D_MODEL), dtype=jnp.float32) * s, 'Wk': jax.random.normal(ks[2], (D_MODEL, D_MODEL), dtype=jnp.float32) * s, 'Wv': jax.random.normal(ks[3], (D_MODEL, VALUE_DIM), dtype=jnp.float32) * s, 'Wg': jax.random.normal(ks[4], (D_MODEL, VALUE_DIM), dtype=jnp.float32) * s, 'Wo': jax.random.normal(ks[5], (VALUE_DIM, D_MODEL), dtype=jnp.float32) * s, 'gn_weight': jnp.ones((HEAD_V,), dtype=jnp.float32)}
    _L0_attn_in = _L0_attn_setup()

    def _L0_ffn_setup():
        import jax, jax.numpy as jnp
        import numpy as np
        DIM = 256
        HIDDEN = 768
        SCALE = 1.0 / 127.0

        def _dequant(w_int, dtype):
            return w_int.astype(dtype) * jnp.asarray(SCALE, dtype)
        key = jax.random.key(seed)
        k_x, k_g, k_u, k_d = jax.random.split(key, 4)
        x = jax.random.normal(k_x, (4, 512, DIM), dtype=jnp.float32)
        w_gate = jax.random.randint(k_g, (HIDDEN, DIM), -127, 128, dtype=jnp.int32)
        w_up = jax.random.randint(k_u, (HIDDEN, DIM), -127, 128, dtype=jnp.int32)
        w_down = jax.random.randint(k_d, (DIM, HIDDEN), -127, 128, dtype=jnp.int32)
        return {'x': x, 'w_gate': w_gate, 'w_up': w_up, 'w_down': w_down}
    _L0_ffn_in = _L0_ffn_setup()
    _d = {'L0_attn_x': _L0_attn_in['x'], 'L0_attn_Wq': _L0_attn_in['Wq'], 'L0_attn_Wk': _L0_attn_in['Wk'], 'L0_attn_Wv': _L0_attn_in['Wv'], 'L0_attn_Wg': _L0_attn_in['Wg'], 'L0_attn_Wo': _L0_attn_in['Wo'], 'L0_attn_gn_weight': _L0_attn_in['gn_weight'], 'L0_ffn_w_gate': _L0_ffn_in['w_gate'], 'L0_ffn_w_up': _L0_ffn_in['w_up'], 'L0_ffn_w_down': _L0_ffn_in['w_down']}
    _x0 = _d['L0_attn_x']
    _d['L0_attn_x'] = jax.random.normal(jax.random.fold_in(jax.random.key(seed), 1), (8, 512, 256), dtype=_x0.dtype)
    del _x0
    return _d

def reference(L0_attn_x, L0_attn_Wq, L0_attn_Wk, L0_attn_Wv, L0_attn_Wg, L0_attn_Wo, L0_attn_gn_weight, L0_ffn_w_gate, L0_ffn_w_up, L0_ffn_w_down):

    def _L0_attn_ref(x, Wq, Wk, Wv, Wg, Wo, gn_weight):
        import jax, jax.numpy as jnp
        import numpy as np
        D_MODEL = 256
        NUM_HEADS = 4
        KEY_DIM = 256
        VALUE_DIM = 512
        HEAD_QK = KEY_DIM // NUM_HEADS
        HEAD_V = VALUE_DIM // NUM_HEADS
        EPS = 1e-05
        CHUNK = 64
        ROPE_BASE = 10000.0

        def apply_rotary(q, k):
            n, d = (q.shape[1], q.shape[-1])
            inv_freq = 1.0 / ROPE_BASE ** (jnp.arange(0, d, 2, dtype=jnp.float32) / d)
            t = jnp.arange(n, dtype=jnp.float32)
            freqs = jnp.outer(t, inv_freq)
            cos = jnp.cos(freqs)[None, :, None, :]
            sin = jnp.sin(freqs)[None, :, None, :]

            def rot(x):
                x1, x2 = jnp.split(x, 2, axis=-1)
                return jnp.concatenate([x1 * cos - x2 * sin, x2 * cos + x1 * sin], axis=-1)
            return (rot(q), rot(k))

        def chunk_retention(q, k, v, gamma, chunk=CHUNK):
            B, H, N, dk = q.shape
            dv = v.shape[-1]
            NC = N // chunk
            qc = jnp.moveaxis(q.reshape(B, H, NC, chunk, dk), 2, 0)
            kc = jnp.moveaxis(k.reshape(B, H, NC, chunk, dk), 2, 0)
            vc = jnp.moveaxis(v.reshape(B, H, NC, chunk, dv), 2, 0)
            idx = jnp.arange(chunk)
            rel = idx[:, None] - idx[None, :]
            D = jnp.where(rel >= 0, gamma[:, None, None] ** rel, 0.0)
            cross_q = (gamma[:, None] ** (idx + 1))[None, :, :, None]
            cross_k = (gamma[:, None] ** (chunk - 1 - idx))[None, :, :, None]
            gC = (gamma ** chunk)[None, :, None, None]

            def step(S, qkv):
                qb, kb, vb = qkv
                attn = jnp.einsum('bhid,bhjd->bhij', qb, kb) * D[None]
                o_intra = jnp.einsum('bhij,bhjd->bhid', attn, vb)
                o_inter = jnp.einsum('bhid,bhde->bhie', qb * cross_q, S)
                S_new = gC * S + jnp.einsum('bhjd,bhje->bhde', kb * cross_k, vb)
                return (S_new, o_intra + o_inter)
            S0 = jnp.zeros((B, H, dk, dv), dtype=q.dtype)
            _, o = jax.lax.scan(step, S0, (qc, kc, vc))
            return jnp.moveaxis(o, 0, 2).reshape(B, H, N, dv)

        def rmsnorm(x, w):
            var = jnp.mean(x * x, axis=-1, keepdims=True)
            return x * jax.lax.rsqrt(var + EPS) * w
        B, N, _ = x.shape
        H = NUM_HEADS
        q1 = (x @ Wq).reshape(B, N, H, HEAD_QK)
        k1 = (x @ Wk).reshape(B, N, H, HEAD_QK)
        q1, k1 = apply_rotary(q1, k1)
        q = jnp.transpose(q1, (0, 2, 1, 3)) * HEAD_QK ** (-0.5)
        k = jnp.transpose(k1, (0, 2, 1, 3))
        v = jnp.transpose((x @ Wv).reshape(B, N, H, HEAD_V), (0, 2, 1, 3))
        gamma = 1.0 - jnp.exp2(-5.0 - jnp.arange(H, dtype=jnp.float32))
        o = chunk_retention(q, k, v, gamma)
        o = jnp.transpose(o, (0, 2, 1, 3))
        o = rmsnorm(o, gn_weight)
        g = jax.nn.silu(x @ Wg)
        o = o.reshape(B, N, VALUE_DIM) * g
        return o @ Wo

    def _L0_ffn_ref(x, w_gate, w_up, w_down):
        import jax, jax.numpy as jnp
        import numpy as np
        DIM = 256
        HIDDEN = 768
        SCALE = 1.0 / 127.0

        def _dequant(w_int, dtype):
            return w_int.astype(dtype) * jnp.asarray(SCALE, dtype)
        wg = _dequant(w_gate, x.dtype)
        wu = _dequant(w_up, x.dtype)
        wd = _dequant(w_down, x.dtype)
        gate = jnp.einsum('bsd,hd->bsh', x, wg)
        up = jnp.einsum('bsd,hd->bsh', x, wu)
        h = jax.nn.silu(gate) * up
        return jnp.einsum('bsh,dh->bsd', h, wd)
    x = L0_attn_x
    x = _layernorm(x + _L0_attn_ref(x, L0_attn_Wq, L0_attn_Wk, L0_attn_Wv, L0_attn_Wg, L0_attn_Wo, L0_attn_gn_weight), axis=-1)
    x = _layernorm(x + _L0_ffn_ref(x, L0_ffn_w_gate, L0_ffn_w_up, L0_ffn_w_down), axis=-1)
    return x

_drawn_inputs = setup_inputs


def setup_inputs(seed=0):
    import zlib

    import numpy as np

    out = dict(_drawn_inputs(seed))
    spreads = {'L0_attn_gn_weight': (1.0, 0.6)}
    factors = {}
    for name, (base, spread) in spreads.items():
        noise = np.random.default_rng([zlib.crc32(name.encode()), seed]).standard_normal(out[name].shape)
        drawn = base * np.exp(spread * noise) if base else spread * noise
        out[name] = jnp.asarray(drawn.astype(out[name].dtype))
    for name, factor in factors.items():
        out[name] = (out[name] * factor).astype(out[name].dtype)
    return out
```

```python
from contextlib import ExitStack

import numpy as np

import concourse.bass as bass
from concourse import mybir

F32 = mybir.dt.float32
F32R = mybir.dt.float32r
I32 = mybir.dt.int32
ALU = mybir.AluOpType
ACT = mybir.ActivationFunctionType

P = 128
D = 256
KD = D // P
H = 4
DK = 64
DV = 128
V = H * DV
HID = 768
HB = HID // P
SEQ = 512
TS = SEQ // P
EPS = 1e-5
ROPE_BASE = 10000.0
SCALE = float(np.float32(1.0 / 127.0))
X1T_LAG, DOWN_LAG = 3, 6
FFN_LAG = 4


def rope_tables():
    f32 = np.float32
    inv_freq = (f32(1.0) / np.power(f32(ROPE_BASE), np.arange(0, DK, 2, dtype=f32) / f32(DK))).astype(f32)
    angle = np.outer(np.arange(SEQ, dtype=f32), inv_freq).astype(f32)
    cos, sin = np.cos(angle).astype(np.float64), np.sin(angle).astype(np.float64)
    gamma = 1.0 - np.exp2(-5.0 - np.arange(H))
    steps = np.arange(SEQ) - SEQ // 2
    decay = np.stack([gamma ** steps[:, None] * DK ** -0.5, gamma ** -steps[:, None]], 1)
    wave = np.stack([np.stack([cos, cos], 1), np.stack([-sin, sin], 1)], 1)
    full = decay[:, None, :, :, None, None] * wave[:, :, None, None]
    full = full.reshape(TS, P, 2, 2 * H * DK).transpose(1, 0, 2, 3)
    return np.ascontiguousarray(full.astype(f32))


def build_block(nc, xT, x, w_proj, w_o, gn, w_ffn, w_down, rope, out):
    tokens = x.shape[0]
    NT = tokens // P
    NSEQ = NT // TS
    LAST = NT + DOWN_LAG + 1
    FIRST_LOOP = 2

    with ExitStack() as ctx:
        def sb(name, shape, dt=F32):
            return ctx.enter_context(nc.sbuf_tensor(name, shape, dt))

        def bank(name):
            return ctx.enter_context(nc.psum_tensor(name, [P, 512], F32))

        def sem(name):
            return ctx.enter_context(nc.semaphore(name))

        wp_hi = sb("wp_hi", [P, 3, KD, 512], F32R)
        wp_lo = sb("wp_lo", [P, 3, KD, 512], F32R)
        wo_raw = sb("wo_raw", [P, H, D])
        wo_hi = sb("wo_hi", [P, H, D], F32R)
        wo_lo = sb("wo_lo", [P, H, D], F32R)
        gn_sb = sb("gn_sb", [P, 1])
        NF = KD * 2 * HID + HB * D
        wf_int = sb("wf_int", [P, NF], I32)
        wp_raw = wf_int[:, 0:3 * KD * 512].bitcast(F32).rearrange("p (c k n) -> p c k n", c=3, k=KD)
        wf_hi = sb("wf_hi", [P, NF], F32R)
        wf_lo = sb("wf_lo", [P, NF], F32R)
        rope_sb = sb("rope_sb", [P, TS, 2, 512])
        ident = sb("ident", [P, P])
        causal = sb("causal", [P, H, P])
        ones = sb("ones", [P, P])
        eps = sb("eps", [P, H])
        half_neg = sb("half_neg", [P, H])
        wide_rows = sb("wide_rows", [P, 1])
        wide_flag = sb("wide_flag", [P, 1], I32)

        def gate_up(w, k, kind, hb):
            at = (k * 2 + kind) * HID + hb * P
            return w[:, at:at + P]

        def down_w(w, hb):
            at = KD * 2 * HID + hb * D
            return w[:, at:at + D]

        xT_raw = sb("xT_raw", [P, 2, KD, 2 * P])
        xT_hi = sb("xT_hi", [P, 2, KD, 2 * P], F32R)
        xT_lo = sb("xT_lo", [P, 2, KD, 2 * P], F32R)
        x_sb = sb("x_sb", [P, 4, D])
        rot_c = sb("rot_c", [P, 512])
        rot_s = sb("rot_s", [P, 512])
        qk = sb("qk", [P, 2, 512])
        kT = sb("kT", [P, 2, 2, P])
        qT = sb("qT", [P, 2, 2, 2, P])
        v_sb = sb("v_sb", [P, 2, V])
        g_sb = sb("g_sb", [P, 2, V])
        attn = sb("attn", [P, 2, H, P])
        state = sb("state", [P, 2, DV])
        sq = sb("sq", [P, P])
        ms = sb("ms", [P, 2, H])
        ms_eps = sb("ms_eps", [P, 2, H])
        rms = sb("rms", [P, 2, H])
        y = sb("y", [P, V])
        yT_hi = sb("yT_hi", [P, V], F32R)
        yT_lo = sb("yT_lo", [P, V], F32R)
        z1 = sb("z1", [P, D])
        st1 = sb("st1", [P, 6])
        mv1 = sb("mv1", [P, 2])
        ve1 = sb("ve1", [P, 1])
        rs1 = sb("rs1", [P, 1])
        x1 = sb("x1", [P, 4, D])
        x1_late = sb("x1_late", [P, 4, D])
        x1T_hi = sb("x1T_hi", [P, 2, KD, 2 * P], F32R)
        x1T_lo = sb("x1T_lo", [P, 2, KD, 2 * P], F32R)
        act_g = sb("act_g", [P, 2, 2 * P])
        h_full = sb("h_full", [P, 2, 2 * P])
        h_hi = sb("h_hi", [P, 2, HB, 2 * P], F32R)
        h_lo = sb("h_lo", [P, 2, HB, 2 * P], F32R)
        z2 = sb("z2", [P, D])
        st2 = sb("st2", [P, 6])
        mv2 = sb("mv2", [P, 2])
        ve2 = sb("ve2", [P, 1])
        rs2 = sb("rs2", [P, 1])
        x2 = sb("x2", [P, 2, D])

        b_rows = [bank("b_rows0"), bank("b_rows1")]
        b_turn = bank("b_turn")
        b_score = bank("b_score")
        b_o = bank("b_o")
        b_state = bank("b_state")
        b_ffn = [bank("b_ffn0"), bank("b_ffn1")]

        wp_in = [sem(f"wp_in{c}") for c in range(3)]
        wo_in, wf_in, gn_in = sem("wo_in"), sem("wf_in"), sem("gn_in")
        rope_in = [sem(f"rope_in{t}") for t in range(TS)]
        xT_in = [sem(f"xT_in{r}") for r in range(2)]
        x_in = [sem(f"x_in{r}") for r in range(2)]
        consts = sem("consts")
        wp_high, wp_split = sem("wp_high"), sem("wp_split")
        wo_scaled, wo_high, wo_split = sem("wo_scaled"), sem("wo_high"), sem("wo_split")
        filled, wf_high, wf_split = sem("filled"), sem("wf_high"), sem("wf_split")
        wide_counted, wide_summed, wide_known = sem("wide_counted"), sem("wide_summed"), sem("wide_known")
        xT_high, xT_split = sem("xT_high"), sem("xT_split")
        qk_done, v_done, g_done = sem("qk_done"), sem("v_done"), sem("g_done")
        rot_parts, rotated = sem("rot_parts"), sem("rotated")
        qkT_done, qkT_copied = sem("qkT_done"), sem("qkT_copied")
        v_copied, g_gated = sem("v_copied"), sem("g_gated")
        scores_done, masked = sem("scores_done"), sem("masked")
        o_done, state_done, state_copied = sem("o_done"), sem("state_done"), sem("state_copied")
        squared, ms_ready, rms_ready, y_ready = sem("squared"), sem("ms_ready"), sem("rms_ready"), sem("y_ready")
        yT_done, yT_high, yT_split = sem("yT_done"), sem("yT_high"), sem("yT_split")
        wo_done, z1_ready, z1_stats, z1_moments = sem("wo_done"), sem("z1_ready"), sem("z1_stats"), sem("z1_moments")
        z1_var, z1_rstd, x1_ready = sem("z1_var"), sem("z1_rstd"), sem("x1_ready")
        x1T_done, x1T_high, x1T_split = sem("x1T_done"), sem("x1T_high"), sem("x1T_split")
        x1_kept = sem("x1_kept")
        ffn_done = [sem(f"ffn_done{j}") for j in range(3)]
        silu_done = [sem(f"silu_done{j}") for j in range(3)]
        h_ready = [sem(f"h_ready{j}") for j in range(3)]
        h_high = [sem(f"h_high{j}") for j in range(3)]
        h_split = [sem(f"h_split{j}") for j in range(3)]
        down_done, z2_ready, z2_stats, z2_moments = sem("down_done"), sem("z2_ready"), sem("z2_stats"), sem("z2_moments")
        z2_var, z2_rstd, x2_ready = sem("z2_var"), sem("z2_rstd"), sem("x2_ready")
        stored = [sem(f"stored{r}") for r in range(2)]

        def exists(n, lo=0):
            return not isinstance(n, int) or lo <= n < NT

        def is_slot(s, n):
            return isinstance(s, int) and s == n

        def ffn_slot(s):
            return not isinstance(s, int) or FFN_LAG <= s < NT + FFN_LAG

        def states_to(q, t):
            return 3 * q + min(t + 1, TS - 1)

        def row_bank(t, k):
            return b_rows[(5 * t + k) % 2]

        def walk(eng, slot, first=0, loop=True):
            for s in range(first, FIRST_LOOP * TS):
                slot(s, s // TS, s % TS)
            with eng.Fori(FIRST_LOOP, NSEQ) as q:
                for t in range(TS):
                    slot(TS * q + t, q, t)
            for s in range(NT, LAST):
                slot(s, s // TS, s % TS)

        def walk_to_last(eng, slot):
            for s in range(FIRST_LOOP * TS):
                slot(s, s // TS, s % TS, s + 2 < NT)
            with eng.Fori(FIRST_LOOP, NSEQ - 1) as q:
                for t in range(TS):
                    slot(TS * q + t, q, t, True)
            for s in range(TS * (NSEQ - 1), LAST):
                slot(s, s // TS, s % TS, s + 2 < NT)

        def back(q, t, lag):
            d = t - lag
            return q + d // TS, d % TS

        block = ctx.enter_context(nc.Block())

        @block.sync
        def _(sp):
            def load_xT(pair, ring):
                sp.dma_start(xT_raw[:, ring], xT[:, :, bass.ds(pair * 2 * P, 2 * P)]).then_inc(xT_in[ring], 16)

            def load_x(pair, ring):
                rows = x[bass.ds(pair * 2 * P, 2 * P), :].rearrange("(a p) d -> p a d", p=P)
                sp.dma_start(x_sb[:, 2 * ring:2 * ring + 2, :], rows).then_inc(x_in[ring], 16)

            load_xT(0, 0)
            sp.dma_start(wp_raw[:, 0], w_proj[:, 0]).then_inc(wp_in[0], 16)
            sp.dma_start(rope_sb[:, 0], rope[:, 0]).then_inc(rope_in[0], 16)
            sp.dma_start(wp_raw[:, 1], w_proj[:, 1]).then_inc(wp_in[1], 16)
            sp.dma_start(wp_raw[:, 2], w_proj[:, 2]).then_inc(wp_in[2], 16)
            sp.dma_start(rope_sb[:, 1], rope[:, 1]).then_inc(rope_in[1], 16)
            load_xT(1, 1)
            sp.dma_start(wo_raw[:], w_o).then_inc(wo_in, 16)
            sp.dma_start(gn_sb[:], gn).then_inc(gn_in, 16)
            load_x(0, 0)
            for t in range(2, TS):
                sp.dma_start(rope_sb[:, t], rope[:, t]).then_inc(rope_in[t], 16)
            load_x(1, 1)
            sp.wait_ge(wp_split, 3)
            sp.dma_start(wf_int[:, 0:KD * 2 * HID], w_ffn).then_inc(wf_in, 16)
            sp.dma_start(wf_int[:, KD * 2 * HID:NF], w_down).then_inc(wf_in, 16)

            def slot(s, q, t):
                if t % 2 == 1:
                    ring = t // 2
                    pair = 2 * q + t // 2 + 2
                    if not isinstance(s, int) or 2 * pair < NT:
                        sp.wait_ge(xT_split, s + 1)
                        load_xT(pair, ring)
                m = s - 3
                if t % 2 == 0 and exists(m) and (not isinstance(s, int) or m + 4 < NT):
                    qm, tm = back(q, t, 3)
                    sp.wait_ge(z1_ready, m + 1)
                    load_x(2 * qm + tm // 2 + 2, tm // 2)
                n = s - DOWN_LAG - 1
                if exists(n):
                    tn = back(q, t, DOWN_LAG + 1)[1]
                    sp.wait_ge(x2_ready, n + 1)
                    sp.dma_start(out[bass.ds(n * P, P), :], x2[:, tn % 2, :]).then_inc(stored[tn % 2], 16)

            for s in range(0, FIRST_LOOP * TS):
                slot(s, s // TS, s % TS)
            with sp.Fori(FIRST_LOOP, NSEQ - 1) as q:
                for t in range(TS):
                    slot(TS * q + t, q, t)
            for s in range(TS * (NSEQ - 1), LAST):
                slot(s, s // TS, s % TS)
            for r in range(2):
                sp.wait_ge(stored[r], 16 * (NT // 2))

        @block.tensor
        def _(pe):
            def wait_bank(s, k, stages):
                n, banks = len(stages), 2 if len(stages) == len(row_stages) else 1
                for d in range(banks, 6 * n, banks):
                    back_slots, stage = divmod(k - d, n)
                    lag, read = stages[stage]
                    m = s + back_slots - lag
                    if exists(m):
                        pe.wait_ge(read, m + 1)
                        return

            row_stages = [(0, rot_parts), (0, v_copied), (0, g_gated), (2, z1_ready), (DOWN_LAG, z2_ready)]
            turn_stages = [(1, qkT_copied), (X1T_LAG, x1T_split), (2, yT_split)]

            def split_product(dst, stat, mov):
                n = len(stat)
                for i in range(n):
                    (sh, sl), (mh, ml) = stat[i], mov[i]
                    passes = [(sh, mh), (sh, ml), (sl, mh)]
                    passes = [p for p in passes if p[0] is not None and p[1] is not None]
                    for j, (a, b) in enumerate(passes):
                        mm = pe.matmul(dst, a, b, start=(i == 0 and j == 0),
                                       stop=(i == n - 1 and j == len(passes) - 1))
                return mm

            def slot(s, q, t, wide):
                now = exists(s)

                n1 = s - 1
                q1, t1 = back(q, t, 1)
                if exists(n1):
                    pe.wait_ge(rotated, n1 + 1)
                    wait_bank(s, 0, turn_stages)
                    for b in range(4):
                        mm = pe.transpose(b_turn[:, b * P:(b + 1) * P], qk[:, t1 % 2, b * P:(b + 1) * P], ident[:])
                    mm.then_inc(qkT_done, 1)

                def project(c, done):
                    ring, at = (t // 2) % 2, (t % 2) * P
                    stat = [(xT_hi[:, ring, k, at:at + P], xT_lo[:, ring, k, at:at + P]) for k in range(KD)]
                    mov = [(wp_hi[:, c, k, :], wp_lo[:, c, k, :]) for k in range(KD)]
                    split_product(row_bank(t, c)[:], stat, mov).then_inc(done, 1)

                if now:
                    pe.wait_ge(xT_split, s + 1)
                    if is_slot(s, 0):
                        pe.wait_ge(wp_split, 1)
                    wait_bank(s, 0, row_stages)
                    project(0, qk_done)

                if now:
                    if is_slot(s, 0):
                        pe.wait_ge(wp_split, 2)
                    wait_bank(s, 1, row_stages)
                    project(1, v_done)

                if exists(n1):
                    pe.wait_ge(qkT_copied, n1 + 1)
                    if exists(n1 - 1):
                        pe.wait_ge(masked, n1)
                    for pr in range(2):
                        mm = pe.matmul(b_score[:, pr * 2 * P:(pr + 1) * 2 * P], kT[:, t1 % 2, pr, :],
                                       qT[:, t1 % 2, pr].rearrange("p a b -> p (a b)"), start=True, stop=True)
                    mm.then_inc(scores_done, 1)

                n3 = s - X1T_LAG
                if exists(n3):
                    q3, t3 = back(q, t, 3)
                    pe.wait_ge(x1_ready, n3 + 1)
                    wait_bank(s, 1, turn_stages)
                    for k in range(KD):
                        mm = pe.transpose(b_turn[:, k * P:(k + 1) * P], x1[:, (t - 3) % 4, k * P:(k + 1) * P], ident[:])
                    mm.then_inc(x1T_done, 1)

                if now:
                    if is_slot(s, 0):
                        pe.wait_ge(wp_split, 3)
                    wait_bank(s, 2, row_stages)
                    project(2, g_done)

                if exists(n1):
                    pe.wait_ge(masked, n1 + 1)
                    pe.wait_ge(v_copied, n1 + 1)
                    if exists(n1 - 1):
                        pe.wait_ge(y_ready, n1)
                    if t1 > 0:
                        pe.wait_ge(state_copied, states_to(q1, t1 - 1))
                    for h in range(H):
                        dst = b_o[:, h * DV:(h + 1) * DV]
                        if t1 > 0:
                            pe.matmul(dst, qT[:, t1 % 2, h // 2, h % 2, :], state[:, h // 2, :], start=True, stop=False)
                        mm = pe.matmul(dst, attn[:, t1 % 2, h, :], v_sb[:, t1 % 2, h * DV:(h + 1) * DV],
                                       start=(t1 == 0), stop=True)
                    mm.then_inc(o_done, 1)
                    if t1 < TS - 1:
                        if t1 == 0 and exists(n1 - 2):
                            pe.wait_ge(state_copied, states_to(q1, t1) - 1)
                        for pr in range(2):
                            mm = pe.matmul(b_state[:, pr * 256:(pr + 1) * 256],
                                           qk[:, t1 % 2, 256 + pr * P:256 + (pr + 1) * P],
                                           v_sb[:, t1 % 2, pr * 256:(pr + 1) * 256],
                                           start=(t1 == 0 and pr == 0), stop=(t1 == TS - 2),
                                           skip_group_check=True)
                        mm.then_inc(state_done, 1)

                n2 = s - 2
                q2, t2 = back(q, t, 2)
                if exists(n2):
                    pe.wait_ge(y_ready, n2 + 1)
                    wait_bank(s, 2, turn_stages)
                    for h in range(H):
                        mm = pe.transpose(b_turn[:, h * P:(h + 1) * P], y[:, h * P:(h + 1) * P], ident[:])
                    mm.then_inc(yT_done, 1)

                def gate_up_block(j):
                    hb = 3 * (t % 2) + j
                    ring = ((t - FFN_LAG) // 2) % 2
                    dst = b_ffn[(3 * t + j) % 2]
                    f = s - FFN_LAG
                    if j == 2:
                        pe.wait_ge(h_ready[0], f + 1)
                    elif exists(f - 1):
                        pe.wait_ge(h_ready[j + 1], f)
                    mov = [(x1T_hi[:, ring, k, :], x1T_lo[:, ring, k, :]) for k in range(KD)]
                    for kind in range(2):
                        stat = [(gate_up(wf_hi, k, kind, hb), gate_up(wf_lo, k, kind, hb) if wide else None)
                                for k in range(KD)]
                        mm = split_product(dst[:, kind * 256:(kind + 1) * 256], stat, mov)
                    mm.then_inc(ffn_done[j], 1)

                if ffn_slot(s):
                    pe.wait_ge(x1T_split, s - 2 if t % 2 == 0 else s - 3)
                    gate_up_block(0)

                if ffn_slot(s):
                    gate_up_block(1)

                if exists(n2):
                    pe.wait_ge(yT_split, n2 + 1)
                    if is_slot(s, 2):
                        pe.wait_ge(wo_split, 1)
                    wait_bank(s, 3, row_stages)
                    stat = [(yT_hi[:, h * P:(h + 1) * P], yT_lo[:, h * P:(h + 1) * P]) for h in range(H)]
                    mov = [(wo_hi[:, h, :], wo_lo[:, h, :]) for h in range(H)]
                    split_product(row_bank(t, 3)[:, 0:D], stat, mov).then_inc(wo_done, 1)

                n6 = s - DOWN_LAG
                if exists(n6):
                    ring, at = ((t - DOWN_LAG) // 2) % 2, (t % 2) * P
                    for j in range(3):
                        pe.wait_ge(h_split[j], s - FFN_LAG if t % 2 == 0 else s - FFN_LAG - 1)
                    wait_bank(s, 4, row_stages)
                    stat = [(h_hi[:, ring, hb, at:at + P], h_lo[:, ring, hb, at:at + P]) for hb in range(HB)]
                    mov = [(down_w(wf_hi, hb), down_w(wf_lo, hb) if wide else None) for hb in range(HB)]
                    split_product(row_bank(t, 4)[:, 0:D], stat, mov).then_inc(down_done, 1)

                if ffn_slot(s):
                    gate_up_block(2)

            pe.wait_ge(consts, 1)
            for s in range(FFN_LAG):
                slot(s, s // TS, s % TS, False)
            pe.wait_ge(wide_counted, 1)
            pe.wait_ge(wf_split, 1)
            pe.matmul(b_ffn[0][:, 0:1], ones[:], wide_rows[:], start=True, stop=True).then_inc(wide_summed, 1)
            pe.wait_ge(wide_known, 1)
            wide = pe.value_load(wide_flag[0:1, 0:1])
            with pe.If(wide != 0):
                walk(pe, lambda s, q, t: slot(s, q, t, True), FFN_LAG)
            with pe.Else():
                walk(pe, lambda s, q, t: slot(s, q, t, False), FFN_LAG)

        @block.scalar
        def _(act):
            def xT_high_part(s, q, t):
                ring, at = t // 2, (t % 2) * P
                act.wait_ge(xT_in[ring], 16 * (q + 1))
                if exists(s - 4):
                    act.wait_ge(g_done, s - 3)
                act.copy(xT_hi[:, ring, :, at:at + P], xT_raw[:, ring, :, at:at + P]).then_inc(xT_high, 1)

            def gate(s, t, j):
                u, f = (3 * t + j) % 2, s - FFN_LAG
                act.wait_ge(ffn_done[j], f + 1)
                if j == 2:
                    act.wait_ge(h_ready[0], f + 1)
                elif exists(f - 1):
                    act.wait_ge(h_ready[j + 1], f)
                act.activation(act_g[:, u], b_ffn[u][:, 0:256], ACT.Silu, scale=SCALE).then_inc(silu_done[j], 1)

            def high(s, t, j):
                hb, u, f = 3 * (t % 2) + j, (3 * t + j) % 2, s - FFN_LAG
                act.wait_ge(h_ready[j], f + 1)
                if exists(f - 4):
                    act.wait_ge(down_done, f - 2 if t % 2 == 0 else f - 3)
                act.copy(h_hi[:, ((t - FFN_LAG) // 2) % 2, hb], h_full[:, u]).then_inc(h_high[j], 1)

            xT_high_part(0, 0, 0)
            xT_high_part(1, 0, 1)
            for c in range(3):
                act.wait_ge(wp_in[c], 16)
                act.copy(wp_hi[:, c], wp_raw[:, c]).then_inc(wp_high, 1)

            def slot(s, q, t, ahead):
                n1, n2, n3 = s - 1, s - 2, s - 3
                q1, t1 = back(q, t, 1)
                if is_slot(s, 2):
                    act.wait_ge(wf_in, 32)
                    act.copy(wf_hi[:], wf_int[:]).then_inc(wf_high, 1)
                if exists(n1):
                    act.wait_ge(qkT_done, n1 + 1)
                    if is_slot(s, 1):
                        act.wait_ge(consts, 1)
                    if exists(n1 - 2):
                        act.wait_ge(o_done, n1 - 1)
                    half = DK
                    src = b_turn[:].rearrange("p (b n) -> p b n", b=4)
                    act.copy(kT[:, t1 % 2], src[:, 2:4, :])
                    for a in range(2):
                        rows = slice(a * half, (a + 1) * half)
                        last = act.copy(qT[rows, t1 % 2, :, a, :], src[rows, 0:2, :])
                    last.then_inc(qkT_copied, 1)
                if ffn_slot(s - 1):
                    high(s - 1, t - 1, 2)
                if ahead:
                    xT_high_part(s + 2, *back(q, t, -2))
                n4 = s - 4
                if exists(n4):
                    t4 = back(q, t, 4)[1]
                    act.wait_ge(x1_ready, n4 + 1)
                    if exists(n4 - 4):
                        act.wait_ge(z2_ready, n4 - 3)
                    act.copy(x1_late[:, t4, :], x1[:, t4, :]).then_inc(x1_kept, 1)
                if exists(s):
                    act.wait_ge(v_done, s + 1)
                    if exists(n2):
                        act.wait_ge(o_done, n2 + 1)
                        q2, t2 = back(q, t, 2)
                        act.wait_ge(state_done, states_to(q2, t2))
                    act.copy(v_sb[:, t % 2], row_bank(t, 1)[:]).then_inc(v_copied, 1)
                if exists(n3):
                    ring, at = ((t - 3) // 2) % 2, ((t - 3) % 2) * P
                    act.wait_ge(x1T_done, n3 + 1)
                    if exists(n3 - 4):
                        act.wait_ge(ffn_done[2], n3 - 2 if (t - 3) % 2 == 0 else n3 - 3)
                    act.copy(x1T_hi[:, ring, :, at:at + P],
                             b_turn[:, 0:KD * P].rearrange("p (k n) -> p k n", k=KD)).then_inc(x1T_high, 1)
                if exists(s):
                    act.wait_ge(g_done, s + 1)
                    if exists(n2):
                        act.wait_ge(y_ready, n2 + 1)
                    act.activation(g_sb[:, t % 2], row_bank(t, 2)[:], ACT.Silu).then_inc(g_gated, 1)
                if exists(n2):
                    act.wait_ge(yT_done, n2 + 1)
                    if exists(n3):
                        act.wait_ge(wo_done, n3 + 1)
                    act.copy(yT_hi[:], b_turn[:]).then_inc(yT_high, 1)
                if exists(n1):
                    act.wait_ge(o_done, n1 + 1)
                    if exists(n1 - 2):
                        act.wait_ge(ms_ready, n1 - 1)
                    for h in range(H):
                        if h > 0 or exists(n1 - 1):
                            act.wait_ge(squared, 4 * n1 + h)
                        act.activation(sq[:], b_o[:, h * DV:(h + 1) * DV], ACT.Square, scale=float(DV) ** -0.5,
                                       accum_out=ms[:, t1 % 2, h:h + 1]).then_inc(squared, 1)
                if exists(n1) and t1 < TS - 1:
                    act.wait_ge(state_done, states_to(q1, t1))
                    for a in range(2):
                        rows = slice(a * DK, (a + 1) * DK)
                        last = act.copy(state[rows], b_state[rows].rearrange("p (c n) -> p c n", c=2)[
                            :, :, a * DV:(a + 1) * DV])
                    last.then_inc(state_copied, 1)
                if ffn_slot(s):
                    gate(s, t, 0)
                    gate(s, t, 1)
                    high(s, t, 0)
                    high(s, t, 1)
                    gate(s, t, 2)

            walk_to_last(act, slot)

        @block.vector
        def _(dve):
            for c in range(3):
                dve.wait_ge(wp_high, c + 1)
                dve.tensor_tensor(wp_lo[:, c], wp_raw[:, c], wp_hi[:, c].bitcast(F32), ALU.subtract).then_inc(wp_split, 1)

            def prepare_wo():
                dve.wait_ge(wo_in, 16)
                dve.wait_ge(gn_in, 16)
                dve.tensor_scalar(wo_raw[:], wo_raw[:], gn_sb[:, 0:1], None, ALU.mult).then_inc(wo_scaled, 1)
                dve.wait_ge(wo_scaled, 1)
                dve.tensor_copy(wo_hi[:], wo_raw[:]).then_inc(wo_high, 1)
                dve.wait_ge(wo_high, 1)
                dve.tensor_tensor(wo_lo[:], wo_raw[:], wo_hi[:].bitcast(F32), ALU.subtract).then_inc(wo_split, 1)

            def count_wide():
                dve.wait_ge(wf_high, 1)
                dve.tensor_tensor(wf_lo[:], wf_int[:], wf_hi[:].bitcast(F32), ALU.subtract).then_inc(wf_split, 1)
                dve.wait_ge(wf_split, 1)
                dve.tensor_scalar(wf_int[:].bitcast(F32), wf_lo[:].bitcast(F32), 0.0, None, ALU.not_equal, ALU.add,
                                  accum_out=wide_rows[:]).then_inc(wide_counted, 1)

            def slot(s, q, t):
                n1, n2, n3, n6 = s - 1, s - 2, s - 3, s - DOWN_LAG
                q1, t1 = back(q, t, 1)
                if is_slot(s, 1):
                    prepare_wo()
                if is_slot(s, 3):
                    count_wide()
                if is_slot(s, 4):
                    dve.wait_ge(wide_summed, 1)
                    dve.tensor_copy(wide_flag[:], b_ffn[0][:, 0:1]).then_inc(wide_known, 1)
                if exists(s):
                    dve.wait_ge(qk_done, s + 1)
                    if isinstance(s, int) and s < TS:
                        dve.wait_ge(rope_in[s], 16)
                    if exists(n1):
                        dve.wait_ge(rotated, n1 + 1)
                    src = row_bank(t, 0)[:]
                    halves = lambda ap: ap.rearrange("p (c e f) -> p c e f", e=2, f=DK // 2)
                    dve.tensor_tensor(rot_c[:], src, rope_sb[:, t, 0, :], ALU.mult)
                    for e in range(2):
                        last = dve.tensor_tensor(halves(rot_s[:])[:, :, e], halves(src)[:, :, 1 - e],
                                                 halves(rope_sb[:, t, 1, :])[:, :, e], ALU.mult)
                    last.then_inc(rot_parts, 1)
                if exists(n3):
                    t3 = back(q, t, 3)[1]
                    dve.wait_ge(z1_rstd, n3 + 1)
                    if exists(n3 - 4):
                        dve.wait_ge(x1_kept, n3 - 3)
                        dve.wait_ge(x1T_done, n3 - 3)
                    dve.tensor_scalar(x1[:, t3, :], z1[:], mv1[:, 0:1], rs1[:, 0:1], ALU.subtract,
                                      ALU.mult).then_inc(x1_ready, 1)
                n7 = s - DOWN_LAG - 1
                if exists(n7):
                    q7, t7 = back(q, t, DOWN_LAG + 1)
                    dve.wait_ge(z2_rstd, n7 + 1)
                    if exists(n7 - 2):
                        dve.wait_ge(stored[t7 % 2], 16 * (2 * q7 + t7 // 2))
                    dve.tensor_scalar(x2[:, t7 % 2, :], z2[:], mv2[:, 0:1], rs2[:, 0:1], ALU.subtract,
                                      ALU.mult).then_inc(x2_ready, 1)
                if exists(s):
                    dve.wait_ge(rot_parts, s + 1)
                    if exists(n2):
                        q2, t2 = back(q, t, 2)
                        dve.wait_ge(qkT_done, n2 + 1)
                        dve.wait_ge(state_done, states_to(q2, t2))
                    dve.tensor_tensor(qk[:, t % 2], rot_c[:], rot_s[:], ALU.add).then_inc(rotated, 1)
                if exists(n1):
                    dve.wait_ge(scores_done, n1 + 1)
                    if is_slot(s, 1):
                        dve.wait_ge(consts, 1)
                    if exists(n1 - 2):
                        dve.wait_ge(o_done, n1 - 1)
                    dve.tensor_tensor(attn[:, t1 % 2].rearrange("p a b -> p (a b)"), b_score[:],
                                      causal[:].rearrange("p a b -> p (a b)"), ALU.mult).then_inc(masked, 1)
                if exists(n3):
                    ring, at = ((t - 3) // 2) % 2, ((t - 3) % 2) * P
                    dve.wait_ge(x1T_high, n3 + 1)
                    dve.tensor_tensor(x1T_lo[:, ring, :, at:at + P],
                                      b_turn[:, 0:KD * P].rearrange("p (k n) -> p k n", k=KD),
                                      x1T_hi[:, ring, :, at:at + P].bitcast(F32), ALU.subtract).then_inc(x1T_split, 1)
                if exists(n2):
                    dve.wait_ge(yT_high, n2 + 1)
                    dve.tensor_tensor(yT_lo[:], b_turn[:], yT_hi[:].bitcast(F32), ALU.subtract).then_inc(yT_split, 1)

                def hidden(j):
                    u, f = (3 * t + j) % 2, s - FFN_LAG
                    dve.wait_ge(silu_done[j], f + 1)
                    if j == 2:
                        dve.wait_ge(h_split[0], f + 1)
                    elif exists(f - 1):
                        dve.wait_ge(h_split[j + 1], f)
                    dve.tensor_tensor(h_full[:, u], b_ffn[u][:, 256:512], act_g[:, u], ALU.mult).then_inc(h_ready[j], 1)

                if ffn_slot(s):
                    hidden(0)
                    hidden(1)
                if exists(n1):
                    dve.wait_ge(rms_ready, n1 + 1)
                    dve.wait_ge(g_gated, n1 + 1)
                    if exists(n1 - 1):
                        dve.wait_ge(yT_done, n1)
                    for h in range(H):
                        cols = slice(h * DV, (h + 1) * DV)
                        last = dve.scalar_tensor_tensor(y[:, cols], b_o[:, cols], rms[:, t1 % 2, h:h + 1],
                                                        g_sb[:, t1 % 2, cols], ALU.mult, ALU.mult)
                    last.then_inc(y_ready, 1)
                if exists(n2):
                    q2, t2 = back(q, t, 2)
                    dve.wait_ge(wo_done, n2 + 1)
                    dve.wait_ge(x_in[t2 // 2], 16 * (q2 + 1))
                    if exists(n3):
                        dve.wait_ge(x1_ready, n3 + 1)
                    dve.tensor_tensor(z1[:], row_bank(t, 3)[:, 0:D], x_sb[:, t2, :], ALU.add).then_inc(z1_ready, 1)
                    dve.wait_ge(z1_ready, n2 + 1)
                    dve.bn_stats(st1[:], z1[:]).then_inc(z1_stats, 1)
                if exists(n6):
                    t6 = back(q, t, DOWN_LAG)[1]
                    dve.wait_ge(down_done, n6 + 1)
                    dve.wait_ge(x1_kept, n6 + 1)
                    if exists(n7):
                        dve.wait_ge(x2_ready, n7 + 1)
                    if exists(n2):
                        dve.wait_ge(z1_stats, n2 + 1)
                    dve.scalar_tensor_tensor(z2[:], row_bank(t, 4)[:, 0:D], SCALE * SCALE, x1_late[:, t6, :],
                                             ALU.mult, ALU.add).then_inc(z2_ready, 1)
                if exists(n2):
                    if not exists(n6):
                        dve.wait_ge(z1_stats, n2 + 1)
                    dve.bn_aggr(mv1[:], st1[:]).then_inc(z1_moments, 1)
                if exists(n6):
                    dve.wait_ge(z2_ready, n6 + 1)
                    dve.bn_stats(st2[:], z2[:]).then_inc(z2_stats, 1)
                    if ffn_slot(s):
                        dve.wait_ge(z2_stats, n6 + 1)
                if ffn_slot(s):
                    hidden(2)
                if exists(n6):
                    if not ffn_slot(s):
                        dve.wait_ge(z2_stats, n6 + 1)
                    dve.bn_aggr(mv2[:], st2[:]).then_inc(z2_moments, 1)

            walk(dve, slot)

        @block.gpsimd
        def _(pool):
            pool.memset(ident[:], 0.0)
            pool.memset(ones[:], 1.0)
            pool.memset(causal[:], 1.0)
            pool.memset(qT[:], 0.0)
            pool.memset(eps[:], EPS)
            pool.memset(half_neg[:], -0.5).then_inc(filled, 1)
            pool.wait_ge(filled, 1)
            pool.affine_select(out=ident[:], in_=ident[:], compare_op=ALU.not_equal, fill=1.0, base=0,
                               pattern=[[-1, P]], channel_multiplier=1)
            pool.affine_select(out=causal[:], in_=causal[:], compare_op=ALU.is_ge, fill=0.0, base=0,
                               pattern=[[0, H], [1, P]], channel_multiplier=-1).then_inc(consts, 1)

            def split_xT(s, q, t):
                ring, at = t // 2, (t % 2) * P
                pool.wait_ge(xT_high, s + 1)
                pool.tensor_tensor(xT_lo[:, ring, :, at:at + P], xT_raw[:, ring, :, at:at + P],
                                   xT_hi[:, ring, :, at:at + P].bitcast(F32), ALU.subtract).then_inc(xT_split, 1)

            def low(s, t, j):
                u, hb = (3 * t + j) % 2, 3 * (t % 2) + j
                ring = ((t - FFN_LAG) // 2) % 2
                pool.wait_ge(h_high[j], s - FFN_LAG + 1)
                pool.tensor_tensor(h_lo[:, ring, hb], h_full[:, u], h_hi[:, ring, hb].bitcast(F32),
                                   ALU.subtract).then_inc(h_split[j], 1)

            split_xT(0, 0, 0)
            split_xT(1, 0, 1)

            def slot(s, q, t, ahead):
                n1, n2, n6 = s - 1, s - 2, s - DOWN_LAG
                q1, t1 = back(q, t, 1)
                if ffn_slot(s - 1):
                    low(s - 1, t - 1, 2)
                if ahead:
                    split_xT(s + 2, *back(q, t, -2))
                if exists(n1):
                    pool.wait_ge(squared, 4 * n1 + 4)
                    if exists(n1 - 2):
                        pool.wait_ge(y_ready, n1 - 1)
                    pool.tensor_tensor(ms_eps[:, t1 % 2], ms[:, t1 % 2], eps[:], ALU.add).then_inc(ms_ready, 1)
                    pool.wait_ge(ms_ready, n1 + 1)
                    pool.tensor_tensor(rms[:, t1 % 2], ms_eps[:, t1 % 2], half_neg[:], ALU.pow).then_inc(rms_ready, 1)

                def inv_std(n, moments, var, rstd, mv, ve, rs):
                    pool.wait_ge(moments, n + 1)
                    pool.tensor_tensor(ve[:], mv[:, 1:2], eps[:, 0:1], ALU.add).then_inc(var, 1)
                    pool.wait_ge(var, n + 1)
                    pool.tensor_tensor(rs[:], ve[:], half_neg[:, 0:1], ALU.pow).then_inc(rstd, 1)

                if ffn_slot(s):
                    low(s, t, 0)
                    low(s, t, 1)
                if exists(n2):
                    inv_std(n2, z1_moments, z1_var, z1_rstd, mv1, ve1, rs1)
                if exists(n6):
                    inv_std(n6, z2_moments, z2_var, z2_rstd, mv2, ve2, rs2)

            walk_to_last(pool, slot)


def kernel(L0_attn_x, L0_attn_Wq, L0_attn_Wk, L0_attn_Wv, L0_attn_Wg, L0_attn_Wo, L0_attn_gn_weight,
           L0_ffn_w_gate, L0_ffn_w_up, L0_ffn_w_down):
    import concourse.bacc as bacc
    from concourse.bass_utils import run_bass_kernel_spmd

    def laid(a):
        return np.ascontiguousarray(np.asarray(a))

    x = laid(L0_attn_x).reshape(-1, D)
    rows = lambda w: w.reshape(-1, P, w.shape[1]).transpose(1, 0, 2)
    proj = np.concatenate([np.asarray(w) for w in (L0_attn_Wq, L0_attn_Wk, L0_attn_Wv, L0_attn_Wg)], 1)
    gate_up = np.concatenate([np.asarray(L0_ffn_w_gate).T, np.asarray(L0_ffn_w_up).T], 1)
    arrays = {
        "in_xT": laid(rows(x.T)),
        "in_x": x,
        "in_w_proj": laid(rows(proj).reshape(P, KD, 3, 512).transpose(0, 2, 1, 3)),
        "in_w_o": laid(rows(np.asarray(L0_attn_Wo))),
        "in_gn": laid(L0_attn_gn_weight).reshape(P, 1),
        "in_w_ffn": laid(rows(gate_up).reshape(P, KD * 2 * HID)),
        "in_w_down": laid(rows(np.asarray(L0_ffn_w_down).T).reshape(P, HB * D)),
        "in_rope": rope_tables(),
    }
    nc = bacc.Bacc("TRN2", target_bir_lowering=False, num_devices=1)
    args = [nc.dram_tensor(n, a.shape, mybir.dt.from_np(a.dtype), kind="ExternalInput").ap()
            for n, a in arrays.items()]
    out = nc.dram_tensor("out_0", x.shape, F32, kind="ExternalOutput").ap()
    build_block(nc, *args, out)
    result = run_bass_kernel_spmd(nc, [arrays], core_ids=[0])
    return result.results[0]["out_0"].reshape(np.asarray(L0_attn_x).shape)
```

```python
from contextlib import ExitStack

import numpy as np

import concourse.bass as bass
from concourse import mybir

F32 = mybir.dt.float32
F32R = mybir.dt.float32r
I32 = mybir.dt.int32
ALU = mybir.AluOpType
ACT = mybir.ActivationFunctionType

P = 128
D = 256
KD = D // P
H = 4
DK = 64
DV = 128
V = H * DV
HID = 768
HB = HID // P
SEQ = 512
TS = SEQ // P
EPS = 1e-5
ROPE_BASE = 10000.0
SCALE = float(np.float32(1.0 / 127.0))
X1T_LAG, DOWN_LAG = 3, 6
WARM_UP = 2
FFN_LAG = 4


def rope_tables():
    f32 = np.float32
    inv_freq = (f32(1.0) / np.power(f32(ROPE_BASE), np.arange(0, DK, 2, dtype=f32) / f32(DK))).astype(f32)
    angle = np.outer(np.arange(SEQ, dtype=f32), inv_freq).astype(f32)
    cos, sin = np.cos(angle).astype(np.float64), np.sin(angle).astype(np.float64)
    gamma = 1.0 - np.exp2(-5.0 - np.arange(H))
    steps = np.arange(SEQ) - SEQ // 2
    decay = np.stack([gamma ** steps[:, None] * DK ** -0.5, gamma ** -steps[:, None]], 1)
    wave = np.stack([np.stack([cos, cos], 1), np.stack([-sin, sin], 1)], 1)
    full = decay[:, None, :, :, None, None] * wave[:, :, None, None]
    full = full.reshape(TS, P, 2, 2 * H * DK).transpose(1, 0, 2, 3)
    return np.ascontiguousarray(full.astype(f32))


def build_block(nc, xT, x, w_proj, w_o, gn, w_ffn, rope, out):
    tokens = x.shape[0]
    NT = tokens // P
    NSEQ = NT // TS
    LAST = NT + DOWN_LAG + 1
    FIRST_LOOP = 2

    with ExitStack() as ctx:
        def sb(name, shape, dt=F32):
            return ctx.enter_context(nc.sbuf_tensor(name, shape, dt))

        def bank(name):
            return ctx.enter_context(nc.psum_tensor(name, [P, 512], F32))

        def sem(name):
            return ctx.enter_context(nc.semaphore(name))

        wp_hi = sb("wp_hi", [P, 3, KD, 512], F32R)
        wp_lo = sb("wp_lo", [P, 3, KD, 512], F32R)
        wo_raw = sb("wo_raw", [P, H, D])
        wo_hi = sb("wo_hi", [P, H, D], F32R)
        wo_lo = sb("wo_lo", [P, H, D], F32R)
        gn_sb = sb("gn_sb", [P, 1])
        NF = KD * 2 * HID + HB * D
        NFP = 6
        wf_int = sb("wf_int", [P, NF], I32)
        wp_raw = wf_int[:, 0:3 * KD * 512].bitcast(F32).rearrange("p (c k n) -> p c k n", c=3, k=KD)
        wf_hi = sb("wf_hi", [P, NF], F32R)
        wf_lo = sb("wf_lo", [P, NF], F32R)
        rope_sb = sb("rope_sb", [P, TS, 2, 512])
        ident = sb("ident", [P, P])
        causal = sb("causal", [P, P])
        ones = sb("ones", [P, P])
        eps = sb("eps", [P, H])
        half_neg = sb("half_neg", [P, H])
        silu_first = sb("silu_first", [P, 1])
        wide_rows = sb("wide_rows", [P, NFP])
        wide_parts = sb("wide_parts", [P, 1])
        wide_flag = sb("wide_flag", [P, 1], I32)

        def ffn_part(c):
            return slice(c * NF // NFP, (c + 1) * NF // NFP)

        def gate_up(w, k, kind, hb):
            at = (k * 2 + kind) * HID + hb * P
            return w[:, at:at + P]

        def down_w(w, hb):
            at = KD * 2 * HID + hb * D
            return w[:, at:at + D]

        xT_raw = sb("xT_raw", [P, 2, KD, 2 * P])
        xT_hi = sb("xT_hi", [P, 2, KD, 2 * P], F32R)
        xT_lo = sb("xT_lo", [P, 2, KD, 2 * P], F32R)
        x_sb = sb("x_sb", [P, 4, D])
        rot_c = sb("rot_c", [P, 512])
        rot_s = sb("rot_s", [P, 512])
        qk = sb("qk", [P, 2, 512])
        qkT_hi = sb("qkT_hi", [P, 4, P], F32R)
        qkT_lo = sb("qkT_lo", [P, 4, P], F32R)
        qdiag_hi = sb("qdiag_hi", [P, 2, 2, P], F32R)
        qdiag_lo = sb("qdiag_lo", [P, 2, 2, P], F32R)
        v_sb = sb("v_sb", [P, 2, V])
        g_sb = sb("g_sb", [P, 2, V])
        k_hi, k_lo = sb("k_hi", [P, 256], F32R), sb("k_lo", [P, 256], F32R)
        v_hi, v_lo = sb("v_hi", [P, V], F32R), sb("v_lo", [P, V], F32R)
        attn = sb("attn", [P, H, P])
        state_hi = sb("state_hi", [P, 2, 2, DV], F32R)
        state_lo = sb("state_lo", [P, 2, 2, DV], F32R)
        sq = sb("sq", [P, P])
        ms = sb("ms", [P, 2, H])
        ms_eps = sb("ms_eps", [P, 2, H])
        rms = sb("rms", [P, 2, H])
        y = sb("y", [P, V])
        yT_hi = sb("yT_hi", [P, V], F32R)
        yT_lo = sb("yT_lo", [P, V], F32R)
        z1 = sb("z1", [P, D])
        st1 = sb("st1", [P, 6])
        mv1 = sb("mv1", [P, 2])
        ve1 = sb("ve1", [P, 1])
        rs1 = sb("rs1", [P, 1])
        x1 = sb("x1", [P, 4, D])
        x1T_hi = sb("x1T_hi", [P, 2, KD, 2 * P], F32R)
        x1T_lo = sb("x1T_lo", [P, 2, KD, 2 * P], F32R)
        h_hi = sb("h_hi", [P, 2, HB, 2 * P], F32R)
        h_lo = sb("h_lo", [P, 2, HB, 2 * P], F32R)
        z2 = wo_raw[:, 0:2, :]
        act_g, h_full, x2, x1_late = (
            wf_int[:, c * 512:(c + n) * 512].bitcast(F32).rearrange("p (r n) -> p r n", r=rings)
            for c, n, rings in ((0, 1, 2), (1, 1, 2), (2, 1, 2), (3, 2, 4)))
        st2 = sb("st2", [P, 2, 6])
        mv2 = sb("mv2", [P, 2, 2])
        ve2 = sb("ve2", [P, 2, 1])
        rs2 = sb("rs2", [P, 2, 1])

        b_rows = [bank("b_rows0"), bank("b_rows1")]
        b_turn = bank("b_turn")
        b_score = bank("b_score")
        b_o = bank("b_o")
        b_state = bank("b_state")
        b_ffn = [bank("b_ffn0"), bank("b_ffn1")]

        wp_in = [sem(f"wp_in{c}") for c in range(3 * KD)]
        wo_in, gn_in = sem("wo_in"), sem("gn_in")
        wf_in = [sem(f"wf_in{c}") for c in range(NFP)]
        rope_in = [sem(f"rope_in{t}") for t in range(TS)]
        xT_in = [sem(f"xT_in{r}") for r in range(2)]
        x_in = [sem(f"x_in{r}") for r in range(2)]
        consts = sem("consts")
        wp_high, wp_split = sem("wp_high"), sem("wp_split")
        wp_split_g = [sem(f"wp_split_g{k}") for k in range(KD)]
        wo_scaled, wo_high, wo_split = sem("wo_scaled"), sem("wo_high"), sem("wo_split")
        filled, wf_high, wf_split = sem("filled"), sem("wf_high"), sem("wf_split")
        low_squared, wide_summed, wide_known = sem("low_squared"), sem("wide_summed"), sem("wide_known")
        xT_high, xT_split = sem("xT_high"), sem("xT_split")
        qk_done, v_done, g_done = sem("qk_done"), sem("v_done"), sem("g_done")
        rot_parts, rotated = sem("rot_parts"), sem("rotated")
        qkT_done, qkT_high, qkT_split = sem("qkT_done"), sem("qkT_high"), sem("qkT_split")
        qdiag_high, qdiag_low = sem("qdiag_high"), sem("qdiag_low")
        v_copied, g_gated = sem("v_copied"), sem("g_gated")
        kv_high, kv_split = sem("kv_high"), sem("kv_split")
        scores_done, masked = sem("scores_done"), sem("masked")
        o_done, state_done = sem("o_done"), sem("state_done")
        state_high, state_split = sem("state_high"), sem("state_split")
        squared, ms_ready, rms_ready, y_ready = sem("squared"), sem("ms_ready"), sem("rms_ready"), sem("y_ready")
        yT_done, yT_high, yT_split = sem("yT_done"), sem("yT_high"), sem("yT_split")
        wo_done, z1_ready, z1_stats, z1_moments = sem("wo_done"), sem("z1_ready"), sem("z1_stats"), sem("z1_moments")
        z1_var, z1_rstd, x1_ready = sem("z1_var"), sem("z1_rstd"), sem("x1_ready")
        x1T_done, x1T_high, x1T_split = sem("x1T_done"), sem("x1T_high"), sem("x1T_split")
        x1_kept = sem("x1_kept")
        ffn_done = [sem(f"ffn_done{j}") for j in range(3)]
        silu_done = [sem(f"silu_done{j}") for j in range(3)]
        h_ready = [sem(f"h_ready{j}") for j in range(3)]
        h_high = [sem(f"h_high{j}") for j in range(3)]
        h_split = [sem(f"h_split{j}") for j in range(3)]
        down_done, z2_ready, z2_stats, z2_moments = sem("down_done"), sem("z2_ready"), sem("z2_stats"), sem("z2_moments")
        z2_var, z2_rstd, x2_ready = sem("z2_var"), sem("z2_rstd"), sem("x2_ready")
        stored = [sem(f"stored{r}") for r in range(2)]

        def exists(n, lo=0):
            return not isinstance(n, int) or lo <= n < NT

        def is_slot(s, n):
            return isinstance(s, int) and s == n

        def ffn_slot(s):
            return not isinstance(s, int) or FFN_LAG <= s < NT + FFN_LAG

        def drained(s):
            return isinstance(s, int) and s > NT

        def sparse(s):
            return isinstance(s, int) and s < 4

        def states_to(q, t):
            return 3 * q + min(t + 1, TS - 1)

        def row_bank(t, k):
            return b_rows[(5 * t + k) % 2]

        def walk(eng, slot):
            for s in range(FIRST_LOOP * TS):
                slot(s, s // TS, s % TS)
            with eng.Fori(FIRST_LOOP, NSEQ) as q:
                for t in range(TS):
                    slot(TS * q + t, q, t)
            for s in range(NT, LAST):
                slot(s, s // TS, s % TS)

        def walk_to_last(eng, slot):
            for s in range(FIRST_LOOP * TS):
                slot(s, s // TS, s % TS, s + 2 < NT)
            with eng.Fori(FIRST_LOOP, NSEQ - 1) as q:
                for t in range(TS):
                    slot(TS * q + t, q, t, True)
            for s in range(TS * (NSEQ - 1), LAST):
                slot(s, s // TS, s % TS, s + 2 < NT)

        def back(q, t, lag):
            d = t - lag
            return q + d // TS, d % TS

        block = ctx.enter_context(nc.Block())

        @block.sync
        def _(sp):
            def load_xT(pair, ring):
                sp.dma_start(xT_raw[:, ring], xT[:, :, bass.ds(pair * 2 * P, 2 * P)]).then_inc(xT_in[ring], 16)

            def load_x(pair, ring):
                rows = x[bass.ds(pair * 2 * P, 2 * P), :].rearrange("(a p) d -> p a d", p=P)
                sp.dma_start(x_sb[:, 2 * ring:2 * ring + 2, :], rows).then_inc(x_in[ring], 16)

            def load_w_proj(c):
                for k in range(KD):
                    sp.dma_start(wp_raw[:, c, k], w_proj[:, c, k]).then_inc(wp_in[KD * c + k], 16)

            load_xT(0, 0)
            load_w_proj(0)
            load_w_proj(1)
            sp.dma_start(rope_sb[:, 0], rope[:, 0]).then_inc(rope_in[0], 16)
            load_w_proj(2)
            sp.dma_start(rope_sb[:, 1], rope[:, 1]).then_inc(rope_in[1], 16)
            load_xT(1, 1)
            sp.dma_start(wo_raw[:], w_o).then_inc(wo_in, 16)
            sp.dma_start(gn_sb[:], gn).then_inc(gn_in, 16)
            load_x(0, 0)
            sp.wait_ge(wp_split, 2 * KD)
            for k in range(KD):
                sp.wait_ge(wp_split_g[k], 1)
            for c in range(NFP):
                if c == 1:
                    sp.wait_ge(xT_split, 2)
                    load_xT(2, 0)
                if c == 2:
                    sp.dma_start(rope_sb[:, 2], rope[:, 2]).then_inc(rope_in[2], 16)
                sp.dma_start(wf_int[:, ffn_part(c)], w_ffn[:, ffn_part(c)]).then_inc(wf_in[c], 16)
            sp.dma_start(rope_sb[:, 3], rope[:, 3]).then_inc(rope_in[3], 16)
            load_x(1, 1)

            def slot(s, q, t):
                if t % 2 == 1 and not is_slot(s, 1):
                    ring = t // 2
                    pair = 2 * q + t // 2 + 2
                    if not isinstance(s, int) or 2 * pair < NT:
                        sp.wait_ge(xT_split, s + 1)
                        load_xT(pair, ring)
                m = s - 3
                if t % 2 == 0 and exists(m) and (not isinstance(s, int) or m + 4 < NT):
                    qm, tm = back(q, t, 3)
                    sp.wait_ge(z1_ready, m + 1)
                    load_x(2 * qm + tm // 2 + 2, tm // 2)
                n = s - DOWN_LAG - 1
                if exists(n):
                    tn = back(q, t, DOWN_LAG + 1)[1]
                    sp.wait_ge(x2_ready, n + 1)
                    sp.dma_start(out[bass.ds(n * P, P), :], x2[:, tn % 2, :]).then_inc(stored[tn % 2], 16)

            for s in range(0, FIRST_LOOP * TS):
                slot(s, s // TS, s % TS)
            with sp.Fori(FIRST_LOOP, NSEQ - 1) as q:
                for t in range(TS):
                    slot(TS * q + t, q, t)
            for s in range(TS * (NSEQ - 1), LAST):
                slot(s, s // TS, s % TS)
            for r in range(2):
                sp.wait_ge(stored[r], 16 * (NT // 2))

        @block.tensor
        def _(pe):
            def wait_bank(s, k, stages):
                n, banks = len(stages), 2 if len(stages) == len(row_stages) else 1
                for d in range(banks, 6 * n, banks):
                    back_slots, stage = divmod(k - d, n)
                    lag, read = stages[stage]
                    m = s + back_slots - lag
                    if exists(m):
                        pe.wait_ge(read, m + 1)
                        return

            row_stages = [(0, rot_parts), (0, v_copied), (0, g_gated), (2, z1_ready), (DOWN_LAG, z2_ready)]
            turn_stages = [(1, qkT_split), (X1T_LAG, x1T_split), (2, yT_split)]

            def split_product(dst, stat, mov, begun=False, more=False):
                n = len(stat)
                for i in range(n):
                    (sh, sl), (mh, ml) = stat[i], mov[i]
                    passes = [(sh, mh), (sh, ml), (sl, mh)]
                    passes = [p for p in passes if p[0] is not None and p[1] is not None]
                    for j, (a, b) in enumerate(passes):
                        mm = pe.matmul(dst, a, b, start=(i == 0 and j == 0 and not begun),
                                       stop=(i == n - 1 and j == len(passes) - 1 and not more),
                                   skip_group_check=begun or more)
                return mm


            def turn_qk(s, q, t):
                n, tn = s - 1, back(q, t, 1)[1]
                if exists(n):
                    pe.wait_ge(rotated, n + 1)
                    wait_bank(s, 0, turn_stages)
                    for b in range(4):
                        mm = pe.transpose(b_turn[:, b * P:(b + 1) * P], qk[:, tn % 2, b * P:(b + 1) * P], ident[:])
                    mm.then_inc(qkT_done, 1)

            def project(s, q, t, c, done):
                if not exists(s):
                    return
                ring, at = (t // 2) % 2, (t % 2) * P
                stat = [(xT_hi[:, ring, k, at:at + P], xT_lo[:, ring, k, at:at + P]) for k in range(KD)]
                mov = [(wp_hi[:, c, k, :], wp_lo[:, c, k, :]) for k in range(KD)]
                if c == 0:
                    pe.wait_ge(xT_split, s + 1)
                wait_bank(s, c, row_stages)
                if is_slot(s, 0):
                    for k in range(KD):
                        if c < 2:
                            pe.wait_ge(wp_split, KD * c + k + 1)
                        else:
                            pe.wait_ge(wp_split_g[k], 1)
                        mm = split_product(row_bank(t, c)[:], stat[k:k + 1], mov[k:k + 1], k > 0, k < KD - 1)
                else:
                    mm = split_product(row_bank(t, c)[:], stat, mov)
                mm.then_inc(done, 1)

            def score(s, q, t):
                n, tn = s - 1, back(q, t, 1)[1]
                if exists(n):
                    pe.wait_ge(qdiag_high, n + 1)
                    pe.wait_ge(qdiag_low, n + 1)
                    if exists(n - 1):
                        pe.wait_ge(masked, n)
                    for pr in range(2):
                        diag = [w[:, pr].rearrange("p a b -> p (a b)") for w in (qdiag_hi, qdiag_lo)]
                        mm = split_product(b_score[:, pr * 2 * P:(pr + 1) * 2 * P],
                                           [(qkT_hi[:, 2 + pr], qkT_lo[:, 2 + pr])], [diag])
                    mm.then_inc(scores_done, 1)

            def turn_x1(s, q, t):
                n, tn = s - X1T_LAG, back(q, t, X1T_LAG)[1]
                if exists(n):
                    pe.wait_ge(x1_ready, n + 1)
                    wait_bank(s, 1, turn_stages)
                    for k in range(KD):
                        mm = pe.transpose(b_turn[:, k * P:(k + 1) * P], x1[:, tn, k * P:(k + 1) * P], ident[:])
                    mm.then_inc(x1T_done, 1)

            def retain(s, q, t):
                n, (qn, tn) = s - 1, back(q, t, 1)
                if not exists(n):
                    return
                pe.wait_ge(masked, n + 1)
                pe.wait_ge(v_copied, n + 1)
                if exists(n - 1):
                    pe.wait_ge(y_ready, n)
                if tn > 0:
                    pe.wait_ge(state_split, states_to(qn, tn - 1))
                for pr in range(2):
                    if tn > 0:
                        mov = [w[:, pr].rearrange("p a b -> p (a b)") for w in (state_hi, state_lo)]
                        split_product(b_o[:, pr * 2 * DV:(pr + 1) * 2 * DV], [(qkT_hi[:, pr], qkT_lo[:, pr])],
                                      [mov], begun=pr > 0, more=True)
                    for h in (2 * pr, 2 * pr + 1):
                        mm = pe.matmul(b_o[:, h * DV:(h + 1) * DV], attn[:, h, :],
                                       v_sb[:, tn % 2, h * DV:(h + 1) * DV],
                                       start=(tn == 0 and h == 0), stop=(h == H - 1), skip_group_check=True)
                mm.then_inc(o_done, 1)

            def update_state(s, q, t):
                n, (qn, tn) = s - 1, back(q, t, 1)
                if exists(n) and tn < TS - 1:
                    if tn == 0 and exists(n - 2):
                        pe.wait_ge(state_split, states_to(qn, tn) - 1)
                    pe.wait_ge(kv_split, states_to(qn, tn))
                    for pr in range(2):
                        cols, vals = slice(pr * P, (pr + 1) * P), slice(pr * 256, (pr + 1) * 256)
                        mm = split_product(b_state[:, vals], [(k_hi[:, cols], k_lo[:, cols])],
                                           [(v_hi[:, vals], v_lo[:, vals])], begun=(tn > 0 or pr > 0),
                                           more=(tn < TS - 2))
                    mm.then_inc(state_done, 1)

            def turn_y(s, q, t):
                n = s - 2
                if exists(n):
                    pe.wait_ge(y_ready, n + 1)
                    wait_bank(s, 2, turn_stages)
                    for h in range(H):
                        mm = pe.transpose(b_turn[:, h * P:(h + 1) * P], y[:, h * P:(h + 1) * P], ident[:])
                    mm.then_inc(yT_done, 1)

            def gate_up_block(s, q, t, j, wide):
                if not ffn_slot(s):
                    return
                f, ring = s - FFN_LAG, ((t - FFN_LAG) // 2) % 2
                hb, dst = 3 * (t % 2) + j, b_ffn[(3 * t + j) % 2]
                if j == 0:
                    pe.wait_ge(x1T_split, s - 2 if t % 2 == 0 else s - 3)
                if j == 2:
                    pe.wait_ge(h_ready[0], f + 1)
                elif exists(f - 1):
                    pe.wait_ge(h_ready[j + 1], f)
                mov = [(x1T_hi[:, ring, k, :], x1T_lo[:, ring, k, :]) for k in range(KD)]
                for kind in range(2):
                    stat = [(gate_up(wf_hi, k, kind, hb), gate_up(wf_lo, k, kind, hb) if wide else None)
                            for k in range(KD)]
                    mm = split_product(dst[:, kind * 256:(kind + 1) * 256], stat, mov)
                mm.then_inc(ffn_done[j], 1)

            def attention_out(s, q, t):
                n = s - 2
                if exists(n):
                    pe.wait_ge(yT_split, n + 1)
                    if is_slot(s, 2):
                        pe.wait_ge(wo_split, 1)
                    wait_bank(s, 3, row_stages)
                    stat = [(yT_hi[:, h * P:(h + 1) * P], yT_lo[:, h * P:(h + 1) * P]) for h in range(H)]
                    mov = [(wo_hi[:, h, :], wo_lo[:, h, :]) for h in range(H)]
                    split_product(row_bank(t, 3)[:, 0:D], stat, mov).then_inc(wo_done, 1)

            def down(s, q, t, wide, parts=(0, 1, 2)):
                n = s - DOWN_LAG
                if not exists(n):
                    return
                ring, at = ((t - DOWN_LAG) // 2) % 2, (t % 2) * P
                if 0 in parts:
                    wait_bank(s, 4, row_stages)
                for j in parts:
                    pe.wait_ge(h_split[j], s - FFN_LAG if t % 2 == 0 else s - FFN_LAG - 1)
                    stat = [(h_hi[:, ring, hb, at:at + P], h_lo[:, ring, hb, at:at + P]) for hb in (j, 3 + j)]
                    mov = [(down_w(wf_hi, hb), down_w(wf_lo, hb) if wide else None) for hb in (j, 3 + j)]
                    mm = split_product(row_bank(t, 4)[:, 0:D], stat, mov, j > 0, j < 2)
                if 2 in parts:
                    mm.then_inc(down_done, 1)

            def sum_wide():
                pe.wait_ge(low_squared, NFP)
                pe.matmul(b_ffn[0][:, 0:NFP], ones[:], wide_rows[:], start=True, stop=True).then_inc(wide_summed, 1)

            def first_half(s, q, t, wide):
                turn_qk(s, q, t)
                project(s, q, t, 0, qk_done)
                gate_up_block(s - 1, q, t - 1, 2, wide)
                project(s, q, t, 1, v_done)
                score(s, q, t)
                project(s, q, t, 2, g_done)
                turn_x1(s, q, t)
                if is_slot(s, 2):
                    turn_y(s, q, t)
                retain(s, q, t)
                if is_slot(s, FFN_LAG):
                    sum_wide()
                if not is_slot(s, 2):
                    turn_y(s, q, t)
                update_state(s, q, t)

            def second_half(s, q, t, wide):
                gate_up_block(s, q, t, 0, wide)
                gate_up_block(s, q, t, 1, wide)
                attention_out(s, q, t)
                down(s, q, t, wide)

            def slot(s, q, t, wide):
                first_half(s, q, t, wide)
                second_half(s, q, t, wide)

            def drain(wide):
                q = NSEQ
                at = lambda t: (NT + t, q, t)
                turn_qk(*at(0))
                gate_up_block(*at(-1), 2, wide)
                down(*at(0), wide, (0, 1))
                score(*at(0))
                turn_x1(*at(0))
                down(*at(0), wide, (2,))
                retain(*at(0))
                turn_y(*at(0))
                gate_up_block(*at(0), 0, wide)
                gate_up_block(*at(0), 1, wide)
                attention_out(*at(0))
                gate_up_block(*at(0), 2, wide)
                gate_up_block(*at(1), 0, wide)
                down(*at(1), wide)
                turn_x1(*at(1))
                gate_up_block(*at(1), 1, wide)
                turn_y(*at(1))
                gate_up_block(*at(1), 2, wide)
                attention_out(*at(1))
                down(*at(2), wide)
                down(*at(3), wide)
                turn_x1(*at(2))
                for t in (2, 3):
                    for j in range(3):
                        gate_up_block(*at(t), j, wide)
                down(*at(4), wide)
                down(*at(5), wide)

            def rest(wide):
                second_half(FFN_LAG, FFN_LAG // TS, FFN_LAG % TS, wide)
                for s in range(FFN_LAG + 1, FIRST_LOOP * TS):
                    slot(s, s // TS, s % TS, wide)
                with pe.Fori(FIRST_LOOP, NSEQ) as q:
                    for t in range(TS):
                        slot(TS * q + t, q, t, wide)
                drain(wide)

            pe.wait_ge(filled, 1)
            for _ in range(WARM_UP):
                pe.matmul(b_ffn[1][:], ones[:], attn[:].rearrange("p a b -> p (a b)"), start=True, stop=True)
            pe.wait_ge(consts, 1)
            for s in range(FFN_LAG):
                slot(s, s // TS, s % TS, False)
            first_half(FFN_LAG, FFN_LAG // TS, FFN_LAG % TS, False)
            pe.wait_ge(wide_known, 2)
            some_wide = pe.value_load(wide_flag[0:1, 0:1])
            with pe.If(some_wide != 0):
                rest(True)
            with pe.Else():
                rest(False)

        @block.scalar
        def _(act):
            def xT_high_part(s, q, t):
                ring, at = t // 2, (t % 2) * P
                act.wait_ge(xT_in[ring], 16 * (q + 1))
                if exists(s - 4):
                    act.wait_ge(g_done, s - 3)
                act.copy(xT_hi[:, ring, :, at:at + P], xT_raw[:, ring, :, at:at + P]).then_inc(xT_high, 1)

            def gate(s, t, j):
                u, f = (3 * t + j) % 2, s - FFN_LAG
                act.wait_ge(ffn_done[j], f + 1)
                if j == 2:
                    act.wait_ge(h_ready[0], f + 1)
                elif exists(f - 1):
                    act.wait_ge(h_ready[j + 1], f)
                act.activation(act_g[:, u], b_ffn[u][:, 0:256], ACT.Silu, scale=SCALE).then_inc(silu_done[j], 1)

            def high(s, t, j):
                hb, u, f = 3 * (t % 2) + j, (3 * t + j) % 2, s - FFN_LAG
                act.wait_ge(h_ready[j], f + 1)
                if exists(f - 4):
                    act.wait_ge(down_done, f - 2 if t % 2 == 0 else f - 3)
                act.copy(h_hi[:, ((t - FFN_LAG) // 2) % 2, hb], h_full[:, u]).then_inc(h_high[j], 1)

            act.wait_ge(filled, 1)
            act.activation(silu_first[:], half_neg[:, 0:1], ACT.Silu)
            xT_high_part(0, 0, 0)
            xT_high_part(1, 0, 1)
            for c in range(3):
                for k in range(KD):
                    act.wait_ge(wp_in[KD * c + k], 16)
                    act.copy(wp_hi[:, c, k], wp_raw[:, c, k]).then_inc(wp_high, 1)
                if c > 0:
                    for diag in ((qdiag_hi, qdiag_lo) if c == 1 else (state_hi, state_lo)):
                        act.copy(diag[:], attn[:].rearrange("p (c a) n -> p c a n", c=2))

            def high_ffn(c):
                act.wait_ge(wf_in[c], 16)
                act.copy(wf_hi[:, ffn_part(c)], wf_int[:, ffn_part(c)]).then_inc(wf_high, 1)

            def high_kv(s, q, t):
                if t < TS - 1:
                    act.wait_ge(rotated, s + 1)
                    act.wait_ge(v_copied, s + 1)
                    if exists(s - 1):
                        act.wait_ge(state_done, states_to(*back(q, t, 1)))
                    act.copy(k_hi[:], qk[:, t % 2, 256:512])
                    act.copy(v_hi[:], v_sb[:, t % 2]).then_inc(kv_high, 1)

            def sum_low_ffn(c):
                act.wait_ge(wf_split, c + 1)
                act.activation(wf_int[:, ffn_part(c)].bitcast(F32), wf_lo[:, ffn_part(c)].bitcast(F32), ACT.Square,
                               accum_out=wide_rows[:, c:c + 1]).then_inc(low_squared, 1)

            def slot(s, q, t, ahead):
                n1, n2, n3 = s - 1, s - 2, s - 3
                q1, t1 = back(q, t, 1)
                if exists(n1):
                    act.wait_ge(qkT_done, n1 + 1)
                    if is_slot(s, 1):
                        act.wait_ge(consts, 1)
                    if exists(n1 - 1):
                        act.wait_ge(o_done, n1)
                    src = b_turn[:].rearrange("p (b n) -> p b n", b=4)
                    act.copy(qkT_hi[:], src).then_inc(qkT_high, 1)
                    act.wait_ge(qkT_high, n1 + 1)
                    for a in range(2):
                        rows = slice(a * DK, (a + 1) * DK)
                        last = act.copy(qdiag_hi[rows, :, a, :], qkT_hi[rows, 0:2, :].bitcast(F32))
                    last.then_inc(qdiag_high, 1)
                    if is_slot(s, NT):
                        gate(s - 1, TS - 1, 2)
                    act.wait_ge(qkT_split, n1 + 1)
                    for a in range(2):
                        rows = slice(a * DK, (a + 1) * DK)
                        last = act.copy(qdiag_lo[rows, :, a, :], qkT_lo[rows, 0:2, :].bitcast(F32))
                    last.then_inc(qdiag_low, 1)
                if exists(n1) and sparse(n1):
                    high_kv(n1, q1, t1)
                if ffn_slot(s - 1) and not drained(s - 1) and not is_slot(s, NT):
                    gate(s - 1, t - 1, 2)
                if ahead:
                    xT_high_part(s + 2, *back(q, t, -2))
                n4 = s - 4
                if exists(n4):
                    t4 = back(q, t, 4)[1]
                    act.wait_ge(x1_ready, n4 + 1)
                    if exists(n4 - 4):
                        act.wait_ge(z2_ready, n4 - 3)
                    act.copy(x1_late[:, t4, :], x1[:, t4, :]).then_inc(x1_kept, 1)
                if exists(s):
                    act.wait_ge(v_done, s + 1)
                    if exists(n2):
                        act.wait_ge(o_done, n2 + 1)
                        q2, t2 = back(q, t, 2)
                        act.wait_ge(kv_split, states_to(q2, t2))
                    act.copy(v_sb[:, t % 2], row_bank(t, 1)[:]).then_inc(v_copied, 1)
                if is_slot(s, 1) or is_slot(s, 2) or is_slot(s, 3):
                    high_ffn((0, 1, 4)[s - 1])
                if ffn_slot(s - 1) and not drained(s - 1):
                    high(s - 1, t - 1, 2)
                if exists(n3):
                    ring, at = ((t - 3) // 2) % 2, ((t - 3) % 2) * P
                    act.wait_ge(x1T_done, n3 + 1)
                    if exists(n3 - 4):
                        act.wait_ge(ffn_done[2], n3 - 2 if (t - 3) % 2 == 0 else n3 - 3)
                    act.copy(x1T_hi[:, ring, :, at:at + P],
                             b_turn[:, 0:KD * P].rearrange("p (k n) -> p k n", k=KD)).then_inc(x1T_high, 1)
                if is_slot(s, FFN_LAG):
                    sum_low_ffn(4)
                    sum_low_ffn(5)
                if exists(s):
                    act.wait_ge(g_done, s + 1)
                    if exists(n2):
                        act.wait_ge(y_ready, n2 + 1)
                    act.activation(g_sb[:, t % 2], row_bank(t, 2)[:], ACT.Silu).then_inc(g_gated, 1)
                if is_slot(s, 2) or is_slot(s, 3):
                    high_ffn(2 if s == 2 else 5)
                if exists(n2) and not is_slot(s, NT + 1):
                    act.wait_ge(yT_done, n2 + 1)
                    if exists(n3):
                        act.wait_ge(wo_done, n3 + 1)
                    act.copy(yT_hi[:], b_turn[:]).then_inc(yT_high, 1)
                if exists(n1):
                    act.wait_ge(o_done, n1 + 1)
                    if exists(n1 - 2):
                        act.wait_ge(ms_ready, n1 - 1)
                    for h in range(H):
                        if h > 0 or exists(n1 - 1):
                            act.wait_ge(squared, 4 * n1 + h)
                        act.activation(sq[:], b_o[:, h * DV:(h + 1) * DV], ACT.Square, scale=float(DV) ** -0.5,
                                       accum_out=ms[:, t1 % 2, h:h + 1]).then_inc(squared, 1)
                if exists(n1) and t1 < TS - 1:
                    act.wait_ge(state_done, states_to(q1, t1))
                    for a in range(2):
                        rows = slice(a * DK, (a + 1) * DK)
                        last = act.copy(state_hi[rows, :, a, :], b_state[rows].rearrange(
                            "p (c n) -> p c n", c=2)[:, :, a * DV:(a + 1) * DV])
                    last.then_inc(state_high, 1)
                if is_slot(s, 2):
                    high_ffn(3)
                    sum_low_ffn(0)
                if is_slot(s, 3):
                    for c in range(1, 4):
                        sum_low_ffn(c)
                if ffn_slot(s):
                    gate(s, t, 0)
                    gate(s, t, 1)
                    if is_slot(s, NT + 1):
                        act.wait_ge(yT_done, n2 + 1)
                        if exists(n3):
                            act.wait_ge(wo_done, n3 + 1)
                        act.copy(yT_hi[:], b_turn[:]).then_inc(yT_high, 1)
                    high(s, t, 0)
                    high(s, t, 1)
                if ffn_slot(s) and drained(s):
                    gate(s, t, 2)
                    high(s, t, 2)
                if exists(s) and not sparse(s):
                    high_kv(s, q, t)

            walk_to_last(act, slot)

        @block.vector
        def _(dve):
            for c in range(2):
                for k in range(KD):
                    dve.wait_ge(wp_high, KD * c + k + 1)
                    dve.tensor_tensor(wp_lo[:, c, k], wp_raw[:, c, k], wp_hi[:, c, k].bitcast(F32),
                                      ALU.subtract).then_inc(wp_split, 1)

            def low_ffn(c):
                part = ffn_part(c)
                dve.wait_ge(wf_high, c + 1)
                dve.tensor_tensor(wf_lo[:, part], wf_int[:, part], wf_hi[:, part].bitcast(F32),
                                  ALU.subtract).then_inc(wf_split, 1)

            def hidden(s, t, j):
                u, f = (3 * t + j) % 2, s - FFN_LAG
                dve.wait_ge(silu_done[j], f + 1)
                if j == 2:
                    dve.wait_ge(h_split[0], f + 1)
                elif exists(f - 1):
                    dve.wait_ge(h_split[j + 1], f)
                dve.tensor_tensor(h_full[:, u], b_ffn[u][:, 256:512], act_g[:, u], ALU.mult).then_inc(h_ready[j], 1)

            def gated_output(n, tn):
                dve.wait_ge(rms_ready, n + 1)
                dve.wait_ge(g_gated, n + 1)
                if exists(n - 1):
                    dve.wait_ge(yT_done, n)
                for h in range(H):
                    cols = slice(h * DV, (h + 1) * DV)
                    last = dve.scalar_tensor_tensor(y[:, cols], b_o[:, cols], rms[:, tn % 2, h:h + 1],
                                                    g_sb[:, tn % 2, cols], ALU.mult, ALU.mult)
                last.then_inc(y_ready, 1)

            def second_norm_of(n, qn, tn):
                r = tn % 2
                dve.wait_ge(z2_rstd, n + 1)
                if exists(n - 2):
                    dve.wait_ge(stored[r], 16 * (2 * qn + tn // 2))
                dve.tensor_scalar(x2[:, r, :], z2[:, r, :], mv2[:, r, 0:1], rs2[:, r, 0:1], ALU.subtract,
                                  ALU.mult).then_inc(x2_ready, 1)

            def residual_first(s):
                return is_slot(s, FFN_LAG) or is_slot(s, FFN_LAG + 1) or is_slot(s, NT)

            def early(s):
                return isinstance(s, int) and 1 <= s < FFN_LAG

            def slot(s, q, t):
                n1, n2, n3, n6, n7 = s - 1, s - 2, s - 3, s - DOWN_LAG, s - DOWN_LAG - 1
                q1, t1 = back(q, t, 1)
                if exists(n1):
                    src = b_turn[:].rearrange("p (b n) -> p b n", b=4)
                    dve.wait_ge(qkT_high, n1 + 1)
                    if exists(n7):
                        dve.wait_ge(z2_stats, n7 + 1)
                    dve.tensor_tensor(qkT_lo[:], src, qkT_hi[:].bitcast(F32), ALU.subtract).then_inc(qkT_split, 1)
                elif exists(n7) and not drained(s - 1):
                    dve.wait_ge(z2_stats, n7 + 1)
                if exists(n7) and not drained(s - 1):
                    r7 = back(q, t, DOWN_LAG + 1)[1] % 2
                    dve.bn_aggr(mv2[:, r7], st2[:, r7]).then_inc(z2_moments, 1)
                if exists(s):
                    dve.wait_ge(qk_done, s + 1)
                    if isinstance(s, int) and s < TS:
                        dve.wait_ge(rope_in[s], 16)
                    if exists(n1):
                        dve.wait_ge(rotated, n1 + 1)
                    src = row_bank(t, 0)[:]
                    halves = lambda ap: ap.rearrange("p (c e f) -> p c e f", e=2, f=DK // 2)
                    dve.tensor_tensor(rot_c[:], src, rope_sb[:, t, 0, :], ALU.mult)
                    for e in range(2):
                        last = dve.tensor_tensor(halves(rot_s[:])[:, :, e], halves(src)[:, :, 1 - e],
                                                 halves(rope_sb[:, t, 1, :])[:, :, e], ALU.mult)
                    last.then_inc(rot_parts, 1)
                if is_slot(s, 0):
                    dve.wait_ge(wp_high, 3 * KD)
                    dve.tensor_tensor(wp_lo[:, 2, 1], wp_raw[:, 2, 1], wp_hi[:, 2, 1].bitcast(F32),
                                      ALU.subtract).then_inc(wp_split_g[1], 1)
                if ffn_slot(s - 1) and not drained(s - 1):
                    hidden(s - 1, t - 1, 2)
                if exists(n3):
                    t3 = back(q, t, 3)[1]
                    dve.wait_ge(z1_rstd, n3 + 1)
                    if exists(n3 - 4):
                        dve.wait_ge(x1_kept, n3 - 3)
                        dve.wait_ge(x1T_done, n3 - 3)
                    dve.tensor_scalar(x1[:, t3, :], z1[:], mv1[:, 0:1], rs1[:, 0:1], ALU.subtract,
                                      ALU.mult).then_inc(x1_ready, 1)
                if exists(n7) and not drained(s):
                    second_norm_of(n7, *back(q, t, DOWN_LAG + 1))
                if early(s - 1):
                    gated_output(n2, n2 % TS)
                if exists(n1):
                    dve.wait_ge(scores_done, n1 + 1)
                    if is_slot(s, 1):
                        dve.wait_ge(consts, 1)
                    if exists(n1 - 1):
                        dve.wait_ge(o_done, n1)
                    dve.tensor_tensor(attn[:], b_score[:].rearrange("p (a b) -> p a b", a=H),
                                      causal[:].unsqueeze(1).broadcast_to((P, H, P)), ALU.mult).then_inc(masked, 1)
                if exists(s):
                    dve.wait_ge(rot_parts, s + 1)
                    if exists(n2):
                        q2, t2 = back(q, t, 2)
                        dve.wait_ge(qkT_done, n2 + 1)
                        dve.wait_ge(kv_split, states_to(q2, t2))
                    dve.tensor_tensor(qk[:, t % 2], rot_c[:], rot_s[:], ALU.add).then_inc(rotated, 1)
                if is_slot(s, 1) or is_slot(s, 2):
                    low_ffn(s - 1)
                if is_slot(s, 1):
                    dve.wait_ge(wo_scaled, 1)
                    dve.tensor_copy(wo_hi[:], wo_raw[:]).then_inc(wo_high, 1)
                    dve.wait_ge(wo_high, 1)
                    dve.tensor_tensor(wo_lo[:], wo_raw[:], wo_hi[:].bitcast(F32), ALU.subtract).then_inc(wo_split, 1)
                if exists(n3):
                    ring, at = ((t - 3) // 2) % 2, ((t - 3) % 2) * P
                    dve.wait_ge(x1T_high, n3 + 1)
                    dve.tensor_tensor(x1T_lo[:, ring, :, at:at + P],
                                      b_turn[:, 0:KD * P].rearrange("p (k n) -> p k n", k=KD),
                                      x1T_hi[:, ring, :, at:at + P].bitcast(F32), ALU.subtract).then_inc(x1T_split, 1)
                if is_slot(s, 3):
                    low_ffn(3)
                    low_ffn(4)
                if is_slot(s, FFN_LAG):
                    dve.wait_ge(wide_summed, 1)
                    dve.tensor_scalar(wide_rows[:], b_ffn[0][:, 0:NFP], 0.0, None, ALU.not_equal, ALU.add,
                                      accum_out=wide_parts[:]).then_inc(wide_known, 1)
                    dve.wait_ge(wide_known, 1)
                    dve.tensor_copy(wide_flag[:], wide_parts[:]).then_inc(wide_known, 1)
                if exists(n2) and not is_slot(s, NT + 1):
                    dve.wait_ge(yT_high, n2 + 1)
                    dve.tensor_tensor(yT_lo[:], b_turn[:], yT_hi[:].bitcast(F32), ALU.subtract).then_inc(yT_split, 1)

                if is_slot(s, 2):
                    low_ffn(2)
                if is_slot(s, 3):
                    low_ffn(5)
                if exists(n1) and t1 < TS - 1:
                    dve.wait_ge(state_high, states_to(q1, t1))
                    for a in range(2):
                        rows = slice(a * DK, (a + 1) * DK)
                        last = dve.tensor_tensor(state_lo[rows, :, a, :], b_state[rows].rearrange(
                            "p (c n) -> p c n", c=2)[:, :, a * DV:(a + 1) * DV],
                            state_hi[rows, :, a, :].bitcast(F32), ALU.subtract)
                    last.then_inc(state_split, 1)
                if ffn_slot(s):
                    hidden(s, t, 0)
                    hidden(s, t, 1)
                if is_slot(s, NT + 1):
                    dve.wait_ge(yT_high, n2 + 1)
                    dve.tensor_tensor(yT_lo[:], b_turn[:], yT_hi[:].bitcast(F32), ALU.subtract).then_inc(yT_split, 1)

                if ffn_slot(s) and drained(s):
                    hidden(s, t, 2)
                if exists(n1) and not early(s) and not residual_first(s):
                    gated_output(n1, t1)
                if exists(n2):
                    q2, t2 = back(q, t, 2)
                    dve.wait_ge(wo_done, n2 + 1)
                    dve.wait_ge(x_in[t2 // 2], 16 * (q2 + 1))
                    if exists(n3):
                        dve.wait_ge(x1_ready, n3 + 1)
                    dve.tensor_tensor(z1[:], row_bank(t, 3)[:, 0:D], x_sb[:, t2, :], ALU.add).then_inc(z1_ready, 1)
                    dve.wait_ge(z1_ready, n2 + 1)
                    dve.bn_stats(st1[:], z1[:]).then_inc(z1_stats, 1)
                if residual_first(s):
                    gated_output(n1, t1)
                if exists(n6):
                    t6 = back(q, t, DOWN_LAG)[1]
                    dve.wait_ge(down_done, n6 + 1)
                    dve.wait_ge(x1_kept, n6 + 1)
                    if exists(n7 - 1):
                        dve.wait_ge(x2_ready, n7)
                    if exists(n2):
                        dve.wait_ge(z1_stats, n2 + 1)
                    dve.scalar_tensor_tensor(z2[:, t6 % 2], row_bank(t, 4)[:, 0:D], SCALE * SCALE, x1_late[:, t6, :],
                                             ALU.mult, ALU.add).then_inc(z2_ready, 1)
                if exists(n2):
                    if not exists(n6):
                        dve.wait_ge(z1_stats, n2 + 1)
                    dve.bn_aggr(mv1[:], st1[:]).then_inc(z1_moments, 1)
                if exists(n6):
                    dve.wait_ge(z2_ready, n6 + 1)
                    dve.bn_stats(st2[:, t6 % 2], z2[:, t6 % 2]).then_inc(z2_stats, 1)
                    if drained(s):
                        dve.wait_ge(z2_stats, n6 + 1)
                        dve.bn_aggr(mv2[:, t6 % 2], st2[:, t6 % 2]).then_inc(z2_moments, 1)
                if exists(n7) and drained(s):
                    second_norm_of(n7, *back(q, t, DOWN_LAG + 1))
            walk(dve, slot)

        @block.gpsimd
        def _(pool):
            pool.memset(ident[:], 0.0)
            pool.memset(ones[:], 1.0)
            pool.memset(causal[:], 1.0)
            pool.memset(attn[:], 0.0)
            pool.memset(eps[:], EPS)
            pool.memset(half_neg[:], -0.5).then_inc(filled, 1)
            pool.wait_ge(filled, 1)
            pool.affine_select(out=ident[:], in_=ident[:], compare_op=ALU.not_equal, fill=1.0, base=0,
                               pattern=[[-1, P]], channel_multiplier=1)
            pool.affine_select(out=causal[:], in_=causal[:], compare_op=ALU.is_ge, fill=0.0, base=0,
                               pattern=[[1, P]], channel_multiplier=-1).then_inc(consts, 1)

            def split_xT(s, q, t):
                ring, at = t // 2, (t % 2) * P
                pool.wait_ge(xT_high, s + 1)
                pool.tensor_tensor(xT_lo[:, ring, :, at:at + P], xT_raw[:, ring, :, at:at + P],
                                   xT_hi[:, ring, :, at:at + P].bitcast(F32), ALU.subtract).then_inc(xT_split, 1)

            def low(s, t, j):
                u, hb = (3 * t + j) % 2, 3 * (t % 2) + j
                ring = ((t - FFN_LAG) // 2) % 2
                pool.wait_ge(h_high[j], s - FFN_LAG + 1)
                pool.tensor_tensor(h_lo[:, ring, hb], h_full[:, u], h_hi[:, ring, hb].bitcast(F32),
                                   ALU.subtract).then_inc(h_split[j], 1)

            def low_kv(q, t):
                if t < TS - 1:
                    pool.wait_ge(kv_high, states_to(q, t))
                    pool.tensor_tensor(k_lo[:], qk[:, t % 2, 256:512], k_hi[:].bitcast(F32), ALU.subtract)
                    pool.tensor_tensor(v_lo[:], v_sb[:, t % 2], v_hi[:].bitcast(F32), ALU.subtract).then_inc(kv_split, 1)

            split_xT(0, 0, 0)
            split_xT(1, 0, 1)
            pool.wait_ge(wp_high, 2 * KD + 1)
            pool.tensor_tensor(wp_lo[:, 2, 0], wp_raw[:, 2, 0], wp_hi[:, 2, 0].bitcast(F32),
                               ALU.subtract).then_inc(wp_split_g[0], 1)

            def slot(s, q, t, ahead):
                n1, n2, n7 = s - 1, s - 2, s - DOWN_LAG - 1
                q1, t1 = back(q, t, 1)

                def inv_std(n, moments, var, rstd, mv, ve, rs):
                    pool.wait_ge(moments, n + 1)
                    pool.tensor_tensor(ve, mv[:, 1:2], eps[:, 0:1], ALU.add).then_inc(var, 1)
                    pool.wait_ge(var, n + 1)
                    pool.tensor_tensor(rs, ve, half_neg[:, 0:1], ALU.pow).then_inc(rstd, 1)

                if exists(n7):
                    r7 = back(q, t, DOWN_LAG + 1)[1] % 2
                    inv_std(n7, z2_moments, z2_var, z2_rstd, mv2[:, r7], ve2[:, r7], rs2[:, r7])
                if exists(n1) and sparse(n1):
                    low_kv(q1, t1)
                if ahead:
                    split_xT(s + 2, *back(q, t, -2))
                if is_slot(s, 0):
                    pool.wait_ge(wo_in, 16)
                    pool.wait_ge(gn_in, 16)
                    pool.tensor_tensor(wo_raw[:].rearrange("p h n -> p (h n)"), wo_raw[:].rearrange("p h n -> p (h n)"),
                                       gn_sb[:, 0:1].broadcast_to((P, H * D)), ALU.mult).then_inc(wo_scaled, 1)
                if ffn_slot(s - 1) and not drained(s - 1):
                    low(s - 1, t - 1, 2)
                if exists(n1):
                    pool.wait_ge(squared, 4 * n1 + 4)
                    if exists(n1 - 2):
                        pool.wait_ge(y_ready, n1 - 1)
                    pool.tensor_tensor(ms_eps[:, t1 % 2], ms[:, t1 % 2], eps[:], ALU.add).then_inc(ms_ready, 1)
                    pool.wait_ge(ms_ready, n1 + 1)
                    pool.tensor_tensor(rms[:, t1 % 2], ms_eps[:, t1 % 2], half_neg[:], ALU.pow).then_inc(rms_ready, 1)

                if ffn_slot(s):
                    low(s, t, 0)
                    low(s, t, 1)
                if ffn_slot(s) and drained(s):
                    low(s, t, 2)
                if exists(s) and not sparse(s):
                    low_kv(q, t)
                if exists(n2):
                    inv_std(n2, z1_moments, z1_var, z1_rstd, mv1[:], ve1[:], rs1[:])

            walk_to_last(pool, slot)


def kernel(L0_attn_x, L0_attn_Wq, L0_attn_Wk, L0_attn_Wv, L0_attn_Wg, L0_attn_Wo, L0_attn_gn_weight,
           L0_ffn_w_gate, L0_ffn_w_up, L0_ffn_w_down):
    import concourse.bacc as bacc
    from concourse.bass_utils import run_bass_kernel_spmd

    def laid(a):
        return np.ascontiguousarray(np.asarray(a))

    x = laid(L0_attn_x).reshape(-1, D)
    rows = lambda w: w.reshape(-1, P, w.shape[1]).transpose(1, 0, 2)
    proj = np.concatenate([np.asarray(w) for w in (L0_attn_Wq, L0_attn_Wk, L0_attn_Wv, L0_attn_Wg)], 1)
    gate_up = np.concatenate([np.asarray(L0_ffn_w_gate).T, np.asarray(L0_ffn_w_up).T], 1)
    arrays = {
        "in_xT": laid(rows(x.T)),
        "in_x": x,
        "in_w_proj": laid(rows(proj).reshape(P, KD, 3, 512).transpose(0, 2, 1, 3)),
        "in_w_o": laid(rows(np.asarray(L0_attn_Wo))),
        "in_gn": laid(L0_attn_gn_weight).reshape(P, 1),
        "in_w_ffn": np.concatenate([rows(gate_up).reshape(P, KD * 2 * HID),
                                    rows(np.asarray(L0_ffn_w_down).T).reshape(P, HB * D)], 1),
        "in_rope": rope_tables(),
    }
    nc = bacc.Bacc("TRN2", target_bir_lowering=False, num_devices=1)
    args = [nc.dram_tensor(n, a.shape, mybir.dt.from_np(a.dtype), kind="ExternalInput").ap()
            for n, a in arrays.items()]
    out = nc.dram_tensor("out_0", x.shape, F32, kind="ExternalOutput").ap()
    build_block(nc, *args, out)
    result = run_bass_kernel_spmd(nc, [arrays], core_ids=[0])
    return result.results[0]["out_0"].reshape(np.asarray(L0_attn_x).shape)
```

```python
from contextlib import ExitStack

import numpy as np

import concourse.bass as bass
from concourse import mybir

F32 = mybir.dt.float32
F32R = mybir.dt.float32r
I32 = mybir.dt.int32
ALU = mybir.AluOpType
ACT = mybir.ActivationFunctionType

P = 128
D = 256
KD = D // P
H = 4
DK = 64
DV = 128
V = H * DV
HID = 768
HB = HID // P
SEQ = 512
TS = SEQ // P
EPS = 1e-5
ROPE_BASE = 10000.0
SCALE = float(np.float32(1.0 / 127.0))
X1T_LAG, DOWN_LAG = 3, 6
WARM_UP = 2
FFN_LAG = 4


def rope_tables():
    f32 = np.float32
    inv_freq = (f32(1.0) / np.power(f32(ROPE_BASE), np.arange(0, DK, 2, dtype=f32) / f32(DK))).astype(f32)
    angle = np.outer(np.arange(SEQ, dtype=f32), inv_freq).astype(f32)
    cos, sin = np.cos(angle).astype(np.float64), np.sin(angle).astype(np.float64)
    gamma = 1.0 - np.exp2(-5.0 - np.arange(H))
    steps = np.arange(SEQ) - SEQ // 2
    decay = np.stack([gamma ** steps[:, None] * DK ** -0.5, gamma ** -steps[:, None]], 1)
    full = decay[:, None, :, :, None] * np.stack([cos, sin], 1)[:, :, None, None]
    full = full.reshape(TS, P, 2, 2 * H, DK // 2).transpose(1, 0, 2, 3, 4)
    return np.ascontiguousarray(full.astype(f32))


def build_block(nc, xT, x, w_proj, w_o, gn, w_ffn, rope, out):
    tokens = x.shape[0]
    NT = tokens // P
    NSEQ = NT // TS
    LAST = NT + DOWN_LAG + 1
    FIRST_LOOP = 2

    with ExitStack() as ctx:
        def sb(name, shape, dt=F32):
            return ctx.enter_context(nc.sbuf_tensor(name, shape, dt))

        def bank(name):
            return ctx.enter_context(nc.psum_tensor(name, [P, 512], F32))

        def sem(name):
            return ctx.enter_context(nc.semaphore(name))

        wp_hi = sb("wp_hi", [P, 3, KD, 512], F32R)
        wp_lo = sb("wp_lo", [P, 3, KD, 512], F32R)
        wo_raw = sb("wo_raw", [P, H, D])
        wo_hi = sb("wo_hi", [P, H, D], F32R)
        wo_lo = sb("wo_lo", [P, H, D], F32R)
        gn_sb = sb("gn_sb", [P, 1])
        NF = KD * 2 * HID + HB * D
        NFP = 6
        wf_int = sb("wf_int", [P, NF], I32)
        wp_raw = wf_int[:, 0:3 * KD * 512].bitcast(F32).rearrange("p (c k n) -> p c k n", c=3, k=KD)
        wf_hi = sb("wf_hi", [P, NF], F32R)
        wf_lo = sb("wf_lo", [P, NF], F32R)
        rope_sb = sb("rope_sb", [P, TS, 2, 2 * H, DK // 2])
        ident = sb("ident", [P, P])
        causal = sb("causal", [P, P])
        ones = sb("ones", [P, P])
        eps = sb("eps", [P, H])
        half_neg = sb("half_neg", [P, H])
        silu_first = sb("silu_first", [P, 1])
        wide_rows = sb("wide_rows", [P, NFP])
        wide_parts = sb("wide_parts", [P, 1])
        wide_flag = sb("wide_flag", [P, 1], I32)

        def ffn_part(c):
            return slice(c * NF // NFP, (c + 1) * NF // NFP)

        def gate_up(w, k, kind, hb):
            at = (k * 2 + kind) * HID + hb * P
            return w[:, at:at + P]

        def down_w(w, hb):
            at = KD * 2 * HID + hb * D
            return w[:, at:at + D]

        xT_raw = sb("xT_raw", [P, 2, KD, 2 * P])
        xT_hi = sb("xT_hi", [P, 2, KD, 2 * P], F32R)
        xT_lo = sb("xT_lo", [P, 2, KD, 2 * P], F32R)
        x_sb = sb("x_sb", [P, 4, D])
        rot_c = sb("rot_c", [P, 512])
        rot_s = sb("rot_s", [P, 512])
        qk = sb("qk", [P, 2, 512])
        qkT_hi = sb("qkT_hi", [P, 4, P], F32R)
        qkT_lo = sb("qkT_lo", [P, 4, P], F32R)
        qdiag_hi = sb("qdiag_hi", [P, 2, 2, P], F32R)
        qdiag_lo = sb("qdiag_lo", [P, 2, 2, P], F32R)
        v_sb = sb("v_sb", [P, 2, V])
        g_sb = sb("g_sb", [P, 2, V])
        k_hi, k_lo = sb("k_hi", [P, 256], F32R), sb("k_lo", [P, 256], F32R)
        v_hi, v_lo = sb("v_hi", [P, V], F32R), sb("v_lo", [P, V], F32R)
        attn = sb("attn", [P, H, P])
        state_hi = sb("state_hi", [P, 2, 2, DV], F32R)
        state_lo = sb("state_lo", [P, 2, 2, DV], F32R)
        sq = sb("sq", [P, P])
        ms = sb("ms", [P, 2, H])
        ms_eps = sb("ms_eps", [P, 2, H])
        rms = sb("rms", [P, 2, H])
        y = sb("y", [P, V])
        yT_hi = sb("yT_hi", [P, V], F32R)
        yT_lo = sb("yT_lo", [P, V], F32R)
        z1 = sb("z1", [P, D])
        st1 = sb("st1", [P, 6])
        mv1 = sb("mv1", [P, 2])
        ve1 = sb("ve1", [P, 1])
        rs1 = sb("rs1", [P, 1])
        x1 = sb("x1", [P, 4, D])
        x1T_hi = sb("x1T_hi", [P, 2, KD, 2 * P], F32R)
        x1T_lo = sb("x1T_lo", [P, 2, KD, 2 * P], F32R)
        h_hi = sb("h_hi", [P, 2, HB, 2 * P], F32R)
        h_lo = sb("h_lo", [P, 2, HB, 2 * P], F32R)
        z2 = wo_raw[:, 0:2, :]
        act_g, h_full, x2, x1_late = (
            wf_int[:, c * 512:(c + n) * 512].bitcast(F32).rearrange("p (r n) -> p r n", r=rings)
            for c, n, rings in ((0, 1, 2), (1, 1, 2), (2, 1, 2), (3, 2, 4)))
        st2 = sb("st2", [P, 2, 6])
        mv2 = sb("mv2", [P, 2, 2])
        ve2 = sb("ve2", [P, 2, 1])
        rs2 = sb("rs2", [P, 2, 1])

        b_rows = [bank("b_rows0"), bank("b_rows1")]
        b_turn = bank("b_turn")
        b_score = bank("b_score")
        b_o = bank("b_o")
        b_state = bank("b_state")
        b_ffn = [bank("b_ffn0"), bank("b_ffn1")]

        wp_in = [sem(f"wp_in{c}") for c in range(3 * KD)]
        wo_in, gn_in = sem("wo_in"), sem("gn_in")
        wf_in = [sem(f"wf_in{c}") for c in range(NFP)]
        rope_in = [sem(f"rope_in{t}") for t in range(TS)]
        xT_in = [sem(f"xT_in{r}") for r in range(2)]
        x_in = [sem(f"x_in{r}") for r in range(2)]
        consts, cleared = sem("consts"), sem("cleared")
        wp_high, wp_split = sem("wp_high"), sem("wp_split")
        wp_split_g = [sem(f"wp_split_g{k}") for k in range(KD)]
        wo_scaled, wo_high, wo_split = sem("wo_scaled"), sem("wo_high"), sem("wo_split")
        filled, wf_high, wf_split = sem("filled"), sem("wf_high"), sem("wf_split")
        low_squared, wide_summed, wide_known = sem("low_squared"), sem("wide_summed"), sem("wide_known")
        xT_high, xT_split = sem("xT_high"), sem("xT_split")
        qk_done, v_done, g_done = sem("qk_done"), sem("v_done"), sem("g_done")
        rot_parts, rotated = sem("rot_parts"), sem("rotated")
        qkT_done, qkT_high, qkT_split = sem("qkT_done"), sem("qkT_high"), sem("qkT_split")
        qdiag_high, qdiag_low = sem("qdiag_high"), sem("qdiag_low")
        v_copied, g_gated = sem("v_copied"), sem("g_gated")
        kv_high, kv_split = sem("kv_high"), sem("kv_split")
        scores_done, masked = sem("scores_done"), sem("masked")
        o_done, state_done = sem("o_done"), sem("state_done")
        state_high, state_split = sem("state_high"), sem("state_split")
        squared, ms_ready, rms_ready, y_ready = sem("squared"), sem("ms_ready"), sem("rms_ready"), sem("y_ready")
        yT_done, yT_high, yT_split = sem("yT_done"), sem("yT_high"), sem("yT_split")
        wo_done, z1_ready, z1_stats, z1_moments = sem("wo_done"), sem("z1_ready"), sem("z1_stats"), sem("z1_moments")
        z1_var, z1_rstd, x1_ready = sem("z1_var"), sem("z1_rstd"), sem("x1_ready")
        x1T_done, x1T_high, x1T_split = sem("x1T_done"), sem("x1T_high"), sem("x1T_split")
        x1_kept = sem("x1_kept")
        ffn_done = [sem(f"ffn_done{j}") for j in range(3)]
        silu_done = [sem(f"silu_done{j}") for j in range(3)]
        h_ready = [sem(f"h_ready{j}") for j in range(3)]
        h_high = [sem(f"h_high{j}") for j in range(3)]
        h_split = [sem(f"h_split{j}") for j in range(3)]
        down_done, z2_ready, z2_stats, z2_moments = sem("down_done"), sem("z2_ready"), sem("z2_stats"), sem("z2_moments")
        z2_var, z2_rstd, x2_ready = sem("z2_var"), sem("z2_rstd"), sem("x2_ready")
        stored = [sem(f"stored{r}") for r in range(2)]

        def exists(n, lo=0):
            return not isinstance(n, int) or lo <= n < NT

        def is_slot(s, n):
            return isinstance(s, int) and s == n

        def ffn_slot(s):
            return not isinstance(s, int) or FFN_LAG <= s < NT + FFN_LAG

        def sparse(s):
            return isinstance(s, int) and 0 <= s < FFN_LAG

        def states_to(q, t):
            return 3 * q + min(t + 1, TS - 1)

        def row_bank(t, k):
            return b_rows[(5 * t + k) % 2]

        def walk_and_drain(eng, slot, drain):
            for s in range(FIRST_LOOP * TS):
                slot(s, s // TS, s % TS, s + 2 < NT)
            with eng.Fori(FIRST_LOOP, NSEQ - 1) as q:
                for t in range(TS):
                    slot(TS * q + t, q, t, True)
            for s in range(NT - TS, NT):
                slot(s, s // TS, s % TS, s + 2 < NT)
            drain()

        def back(q, t, lag):
            d = t - lag
            return q + d // TS, d % TS

        block = ctx.enter_context(nc.Block())

        @block.sync
        def _(sp):
            def load_xT(pair, ring):
                sp.dma_start(xT_raw[:, ring], xT[:, :, bass.ds(pair * 2 * P, 2 * P)]).then_inc(xT_in[ring], 16)

            def load_x(pair, ring):
                rows = x[bass.ds(pair * 2 * P, 2 * P), :].rearrange("(a p) d -> p a d", p=P)
                sp.dma_start(x_sb[:, 2 * ring:2 * ring + 2, :], rows).then_inc(x_in[ring], 16)

            def load_w_proj(c):
                for k in range(KD):
                    sp.dma_start(wp_raw[:, c, k], w_proj[:, c, k]).then_inc(wp_in[KD * c + k], 16)

            load_xT(0, 0)
            load_w_proj(0)
            load_w_proj(1)
            sp.dma_start(rope_sb[:, 0], rope[:, 0]).then_inc(rope_in[0], 16)
            load_w_proj(2)
            sp.dma_start(rope_sb[:, 1], rope[:, 1]).then_inc(rope_in[1], 16)
            load_xT(1, 1)
            sp.dma_start(wo_raw[:], w_o).then_inc(wo_in, 16)
            sp.dma_start(gn_sb[:], gn).then_inc(gn_in, 16)
            load_x(0, 0)
            sp.wait_ge(wp_split, 2 * KD)
            for k in range(KD):
                sp.wait_ge(wp_split_g[k], 1)
            for c in range(NFP):
                if c == 1:
                    sp.wait_ge(xT_split, 2)
                    load_xT(2, 0)
                if c == 2:
                    sp.dma_start(rope_sb[:, 2], rope[:, 2]).then_inc(rope_in[2], 16)
                sp.dma_start(wf_int[:, ffn_part(c)], w_ffn[:, ffn_part(c)]).then_inc(wf_in[c], 16)
            sp.dma_start(rope_sb[:, 3], rope[:, 3]).then_inc(rope_in[3], 16)
            load_x(1, 1)

            def slot(s, q, t):
                if t % 2 == 1 and not is_slot(s, 1):
                    ring = t // 2
                    pair = 2 * q + t // 2 + 2
                    if not isinstance(s, int) or 2 * pair < NT:
                        sp.wait_ge(xT_split, s + 1)
                        load_xT(pair, ring)
                m = s - 3
                if t % 2 == 0 and exists(m) and (not isinstance(s, int) or m + 4 < NT):
                    qm, tm = back(q, t, 3)
                    sp.wait_ge(z1_ready, m + 1)
                    load_x(2 * qm + tm // 2 + 2, tm // 2)
                n = s - DOWN_LAG - 1
                if exists(n):
                    tn = back(q, t, DOWN_LAG + 1)[1]
                    sp.wait_ge(x2_ready, n + 1)
                    sp.dma_start(out[bass.ds(n * P, P), :], x2[:, tn % 2, :]).then_inc(stored[tn % 2], 16)

            def drain():
                for s in range(NT, LAST):
                    slot(s, s // TS, s % TS)
                for r in range(2):
                    sp.wait_ge(stored[r], 16 * (NT // 2))

            walk_and_drain(sp, lambda s, q, t, ahead: slot(s, q, t), drain)

        @block.tensor
        def _(pe):
            def wait_bank(s, k, stages):
                n, banks = len(stages), 2 if len(stages) == len(row_stages) else 1
                for d in range(banks, 6 * n, banks):
                    back_slots, stage = divmod(k - d, n)
                    lag, read = stages[stage]
                    m = s + back_slots - lag
                    if exists(m):
                        pe.wait_ge(read, m + 1)
                        return

            row_stages = [(0, rot_parts), (0, v_copied), (0, g_gated), (2, z1_ready), (DOWN_LAG, z2_ready)]
            turn_stages = [(1, qkT_split), (X1T_LAG, x1T_split), (2, yT_split)]

            def split_product(dst, stat, mov, begun=False, more=False):
                n = len(stat)
                for i in range(n):
                    (sh, sl), (mh, ml) = stat[i], mov[i]
                    passes = [(sh, mh), (sh, ml), (sl, mh)]
                    passes = [p for p in passes if p[0] is not None and p[1] is not None]
                    for j, (a, b) in enumerate(passes):
                        mm = pe.matmul(dst, a, b, start=(i == 0 and j == 0 and not begun),
                                       stop=(i == n - 1 and j == len(passes) - 1 and not more),
                                   skip_group_check=begun or more)
                return mm


            def turn_qk(s, q, t):
                n, tn = s - 1, back(q, t, 1)[1]
                if exists(n):
                    pe.wait_ge(rotated, n + 1)
                    wait_bank(s, 0, turn_stages)
                    for b in range(4):
                        mm = pe.transpose(b_turn[:, b * P:(b + 1) * P], qk[:, tn % 2, b * P:(b + 1) * P], ident[:])
                    mm.then_inc(qkT_done, 1)

            def project(s, q, t, c, done):
                if not exists(s):
                    return
                ring, at = (t // 2) % 2, (t % 2) * P
                stat = [(xT_hi[:, ring, k, at:at + P], xT_lo[:, ring, k, at:at + P]) for k in range(KD)]
                mov = [(wp_hi[:, c, k, :], wp_lo[:, c, k, :]) for k in range(KD)]
                if c == 0:
                    pe.wait_ge(xT_split, s + 1)
                wait_bank(s, c, row_stages)
                if is_slot(s, 0):
                    for k in range(KD):
                        if c < 2:
                            pe.wait_ge(wp_split, KD * c + k + 1)
                        else:
                            pe.wait_ge(wp_split_g[k], 1)
                        mm = split_product(row_bank(t, c)[:], stat[k:k + 1], mov[k:k + 1], k > 0, k < KD - 1)
                else:
                    mm = split_product(row_bank(t, c)[:], stat, mov)
                mm.then_inc(done, 1)

            def score(s, q, t):
                n, tn = s - 1, back(q, t, 1)[1]
                if exists(n):
                    pe.wait_ge(qdiag_high, n + 1)
                    pe.wait_ge(qdiag_low, n + 1)
                    if exists(n - 1):
                        pe.wait_ge(masked, n)
                    for pr in range(2):
                        diag = [w[:, pr].rearrange("p a b -> p (a b)") for w in (qdiag_hi, qdiag_lo)]
                        mm = split_product(b_score[:, pr * 2 * P:(pr + 1) * 2 * P],
                                           [(qkT_hi[:, 2 + pr], qkT_lo[:, 2 + pr])], [diag])
                    mm.then_inc(scores_done, 1)

            def turn_x1(s, q, t, free=None):
                n, tn = s - X1T_LAG, back(q, t, X1T_LAG)[1]
                if exists(n):
                    pe.wait_ge(x1_ready, n + 1)
                    if free:
                        pe.wait_ge(*free)
                    else:
                        wait_bank(s, 1, turn_stages)
                    for k in range(KD):
                        mm = pe.transpose(b_turn[:, k * P:(k + 1) * P], x1[:, tn, k * P:(k + 1) * P], ident[:])
                    mm.then_inc(x1T_done, 1)

            def retain(s, q, t):
                n, (qn, tn) = s - 1, back(q, t, 1)
                if not exists(n):
                    return
                pe.wait_ge(masked, n + 1)
                pe.wait_ge(v_copied, n + 1)
                if exists(n - 1):
                    pe.wait_ge(y_ready, n)
                if tn > 0:
                    pe.wait_ge(state_split, states_to(qn, tn - 1))
                for pr in range(2):
                    if tn > 0:
                        mov = [w[:, pr].rearrange("p a b -> p (a b)") for w in (state_hi, state_lo)]
                        split_product(b_o[:, pr * 2 * DV:(pr + 1) * 2 * DV], [(qkT_hi[:, pr], qkT_lo[:, pr])],
                                      [mov], begun=pr > 0, more=True)
                    for h in (2 * pr, 2 * pr + 1):
                        mm = pe.matmul(b_o[:, h * DV:(h + 1) * DV], attn[:, h, :],
                                       v_sb[:, tn % 2, h * DV:(h + 1) * DV],
                                       start=(tn == 0 and h == 0), stop=(h == H - 1), skip_group_check=True)
                mm.then_inc(o_done, 1)

            def update_state(s, q, t):
                n, (qn, tn) = s - 1, back(q, t, 1)
                if exists(n) and tn < TS - 1:
                    if tn == 0 and exists(n - 2):
                        pe.wait_ge(state_split, states_to(qn, tn) - 1)
                    pe.wait_ge(kv_split, states_to(qn, tn))
                    for pr in range(2):
                        cols, vals = slice(pr * P, (pr + 1) * P), slice(pr * 256, (pr + 1) * 256)
                        mm = split_product(b_state[:, vals], [(k_hi[:, cols], k_lo[:, cols])],
                                           [(v_hi[:, vals], v_lo[:, vals])], begun=(tn > 0 or pr > 0),
                                           more=(tn < TS - 2))
                    mm.then_inc(state_done, 1)

            def turn_y(s, q, t, free=None):
                n = s - 2
                if exists(n):
                    pe.wait_ge(y_ready, n + 1)
                    if free:
                        pe.wait_ge(*free)
                    else:
                        wait_bank(s, 2, turn_stages)
                    for h in range(H):
                        mm = pe.transpose(b_turn[:, h * P:(h + 1) * P], y[:, h * P:(h + 1) * P], ident[:])
                    mm.then_inc(yT_done, 1)

            def gate_up_block(s, q, t, j, wide):
                if not ffn_slot(s):
                    return
                f, ring = s - FFN_LAG, ((t - FFN_LAG) // 2) % 2
                hb, dst = 3 * (t % 2) + j, b_ffn[(3 * t + j) % 2]
                if j == 0:
                    pe.wait_ge(x1T_split, s - 2 if t % 2 == 0 else s - 3)
                if j == 2:
                    pe.wait_ge(h_ready[0], f + 1)
                elif exists(f - 1):
                    pe.wait_ge(h_ready[j + 1], f)
                mov = [(x1T_hi[:, ring, k, :], x1T_lo[:, ring, k, :]) for k in range(KD)]
                for kind in range(2):
                    stat = [(gate_up(wf_hi, k, kind, hb), gate_up(wf_lo, k, kind, hb) if wide else None)
                            for k in range(KD)]
                    mm = split_product(dst[:, kind * 256:(kind + 1) * 256], stat, mov)
                mm.then_inc(ffn_done[j], 1)

            def attention_out(s, q, t):
                n = s - 2
                if exists(n):
                    pe.wait_ge(yT_split, n + 1)
                    if is_slot(s, 2):
                        pe.wait_ge(wo_split, 1)
                    wait_bank(s, 3, row_stages)
                    stat = [(yT_hi[:, h * P:(h + 1) * P], yT_lo[:, h * P:(h + 1) * P]) for h in range(H)]
                    mov = [(wo_hi[:, h, :], wo_lo[:, h, :]) for h in range(H)]
                    split_product(row_bank(t, 3)[:, 0:D], stat, mov).then_inc(wo_done, 1)

            def down(s, q, t, wide, parts=(0, 1, 2)):
                n = s - DOWN_LAG
                if not exists(n):
                    return
                ring, at = ((t - DOWN_LAG) // 2) % 2, (t % 2) * P
                if 0 in parts:
                    wait_bank(s, 4, row_stages)
                for j in parts:
                    pe.wait_ge(h_split[j], s - FFN_LAG if t % 2 == 0 else s - FFN_LAG - 1)
                    stat = [(h_hi[:, ring, hb, at:at + P], h_lo[:, ring, hb, at:at + P]) for hb in (j, 3 + j)]
                    mov = [(down_w(wf_hi, hb), down_w(wf_lo, hb) if wide else None) for hb in (j, 3 + j)]
                    mm = split_product(row_bank(t, 4)[:, 0:D], stat, mov, j > 0, j < 2)
                if 2 in parts:
                    mm.then_inc(down_done, 1)

            def sum_wide():
                pe.wait_ge(low_squared, NFP)
                pe.matmul(b_ffn[0][:, 0:NFP], ones[:], wide_rows[:], start=True, stop=True).then_inc(wide_summed, 1)

            def first_half(s, q, t, wide):
                turn_qk(s, q, t)
                project(s, q, t, 0, qk_done)
                gate_up_block(s - 1, q, t - 1, 2, wide)
                project(s, q, t, 1, v_done)
                score(s, q, t)
                project(s, q, t, 2, g_done)
                turn_x1(s, q, t)
                if is_slot(s, 2):
                    turn_y(s, q, t)
                retain(s, q, t)
                if is_slot(s, FFN_LAG):
                    sum_wide()
                if not is_slot(s, 2):
                    turn_y(s, q, t)
                update_state(s, q, t)

            def second_half(s, q, t, wide):
                gate_up_block(s, q, t, 0, wide)
                gate_up_block(s, q, t, 1, wide)
                attention_out(s, q, t)
                down(s, q, t, wide)

            def slot(s, q, t, wide):
                first_half(s, q, t, wide)
                second_half(s, q, t, wide)

            def last_slot(wide):
                s, q, t = NT - 1, NSEQ - 1, TS - 1
                first_half(s, q, t, wide)
                gate_up_block(s, q, t, 0, wide)
                turn_qk(NT, NSEQ, 0)
                attention_out(s, q, t)
                gate_up_block(s, q, t, 1, wide)
                down(s, q, t, wide, (0,))
                score(NT, NSEQ, 0)
                down(s, q, t, wide, (1, 2))
                turn_y(NT, NSEQ, 0, free=(qkT_split, NT))
                retain(NT, NSEQ, 0)

            def drain(wide):
                q = NSEQ
                at = lambda t: (NT + t, q, t)
                gate_up_block(*at(-1), 2, wide)
                turn_x1(*at(0), free=(yT_split, NT - 1))
                down(*at(0), wide, (0, 1))
                attention_out(*at(0))
                down(*at(0), wide, (2,))
                turn_y(*at(1), free=(x1T_split, NT - 2))
                gate_up_block(*at(0), 0, wide)
                gate_up_block(*at(0), 1, wide)
                attention_out(*at(1))
                gate_up_block(*at(0), 2, wide)
                gate_up_block(*at(1), 0, wide)
                turn_x1(*at(1), free=(yT_split, NT))
                down(*at(1), wide)
                gate_up_block(*at(1), 1, wide)
                turn_x1(*at(2), free=(x1T_split, NT - 1))
                gate_up_block(*at(1), 2, wide)
                down(*at(2), wide, (0,))
                gate_up_block(*at(2), 0, wide)
                down(*at(2), wide, (1, 2))
                gate_up_block(*at(2), 1, wide)
                gate_up_block(*at(2), 2, wide)
                down(*at(3), wide, (0,))
                gate_up_block(*at(3), 0, wide)
                down(*at(3), wide, (1, 2))
                gate_up_block(*at(3), 1, wide)
                gate_up_block(*at(3), 2, wide)
                down(*at(4), wide, (0, 1))
                down(*at(5), wide, (0, 1))
                down(*at(4), wide, (2,))
                down(*at(5), wide, (2,))

            def rest(wide):
                second_half(FFN_LAG, FFN_LAG // TS, FFN_LAG % TS, wide)
                for s in range(FFN_LAG + 1, FIRST_LOOP * TS):
                    slot(s, s // TS, s % TS, wide)
                with pe.Fori(FIRST_LOOP, NSEQ - 1) as q:
                    for t in range(TS):
                        slot(TS * q + t, q, t, wide)
                for s in range(NT - TS, NT - 1):
                    slot(s, s // TS, s % TS, wide)
                last_slot(wide)
                drain(wide)

            pe.wait_ge(filled, 1)
            for _ in range(WARM_UP):
                pe.matmul(b_ffn[1][:], ones[:], attn[:].rearrange("p a b -> p (a b)"), start=True, stop=True)
            pe.wait_ge(consts, 1)
            for s in range(FFN_LAG):
                slot(s, s // TS, s % TS, False)
            first_half(FFN_LAG, FFN_LAG // TS, FFN_LAG % TS, False)
            pe.wait_ge(wide_known, 2)
            some_wide = pe.value_load(wide_flag[0:1, 0:1])
            with pe.If(some_wide != 0):
                rest(True)
            with pe.Else():
                rest(False)

        @block.scalar
        def _(act):
            def split_xT(s, q, t):
                ring, at = t // 2, (t % 2) * P
                act.wait_ge(xT_in[ring], 16 * (q + 1))
                if exists(s - 4):
                    act.wait_ge(g_done, s - 3)
                act.copy(xT_hi[:, ring, :, at:at + P], xT_raw[:, ring, :, at:at + P]).then_inc(xT_high, 1)

            def split_qk(s, q, t, between=None):
                n = s - 1
                if not exists(n):
                    return
                act.wait_ge(qkT_done, n + 1)
                if is_slot(s, 1):
                    act.wait_ge(cleared, 1)
                if exists(n - 1):
                    act.wait_ge(o_done, n)
                act.copy(qkT_hi[:], b_turn[:].rearrange("p (b n) -> p b n", b=4)).then_inc(qkT_high, 1)
                act.wait_ge(qkT_high, n + 1)
                for a in range(2):
                    rows = slice(a * DK, (a + 1) * DK)
                    last = act.copy(qdiag_hi[rows, :, a, :], qkT_hi[rows, 0:2, :].bitcast(F32))
                last.then_inc(qdiag_high, 1)
                if between:
                    between()
                act.wait_ge(qkT_split, n + 1)
                for a in range(2):
                    rows = slice(a * DK, (a + 1) * DK)
                    last = act.copy(qdiag_lo[rows, :, a, :], qkT_lo[rows, 0:2, :].bitcast(F32))
                last.then_inc(qdiag_low, 1)

            def keep_x1(s, q, t):
                n, tn = s - 4, back(q, t, 4)[1]
                if exists(n):
                    act.wait_ge(x1_ready, n + 1)
                    if exists(n - 4):
                        act.wait_ge(z2_ready, n - 3)
                    act.copy(x1_late[:, tn, :], x1[:, tn, :]).then_inc(x1_kept, 1)

            def copy_v(s, q, t):
                if exists(s):
                    act.wait_ge(v_done, s + 1)
                    if exists(s - 2):
                        act.wait_ge(o_done, s - 1)
                        act.wait_ge(kv_split, states_to(*back(q, t, 2)))
                    act.copy(v_sb[:, t % 2], row_bank(t, 1)[:]).then_inc(v_copied, 1)

            def split_kv(s, q, t):
                if exists(s) and t < TS - 1:
                    act.wait_ge(rotated, s + 1)
                    act.wait_ge(v_copied, s + 1)
                    if exists(s - 1):
                        act.wait_ge(state_done, states_to(*back(q, t, 1)))
                    act.copy(k_hi[:], qk[:, t % 2, 256:512])
                    act.copy(v_hi[:], v_sb[:, t % 2]).then_inc(kv_high, 1)

            def split_x1T(s, q, t):
                n = s - X1T_LAG
                if exists(n):
                    ring, at = ((t - 3) // 2) % 2, ((t - 3) % 2) * P
                    act.wait_ge(x1T_done, n + 1)
                    if exists(n - 4):
                        act.wait_ge(ffn_done[2], n - 2 if (t - 3) % 2 == 0 else n - 3)
                    act.copy(x1T_hi[:, ring, :, at:at + P],
                             b_turn[:, 0:KD * P].rearrange("p (k n) -> p k n", k=KD)).then_inc(x1T_high, 1)

            def gate_v(s, q, t):
                if exists(s):
                    act.wait_ge(g_done, s + 1)
                    if exists(s - 2):
                        act.wait_ge(y_ready, s - 1)
                    act.activation(g_sb[:, t % 2], row_bank(t, 2)[:], ACT.Silu).then_inc(g_gated, 1)

            def split_y(s, q, t):
                n = s - 2
                if exists(n):
                    act.wait_ge(yT_done, n + 1)
                    if exists(n - 1):
                        act.wait_ge(wo_done, n)
                    act.copy(yT_hi[:], b_turn[:]).then_inc(yT_high, 1)

            def mean_squares(s, q, t):
                n, tn = s - 1, back(q, t, 1)[1]
                if exists(n):
                    act.wait_ge(o_done, n + 1)
                    if exists(n - 2):
                        act.wait_ge(ms_ready, n - 1)
                    for h in range(H):
                        if h > 0 or exists(n - 1):
                            act.wait_ge(squared, 4 * n + h)
                        act.activation(sq[:], b_o[:, h * DV:(h + 1) * DV], ACT.Square, scale=float(DV) ** -0.5,
                                       accum_out=ms[:, tn % 2, h:h + 1]).then_inc(squared, 1)

            def split_state(s, q, t):
                qn, tn = back(q, t, 1)
                if exists(s - 1) and tn < TS - 1:
                    act.wait_ge(state_done, states_to(qn, tn))
                    for a in range(2):
                        rows = slice(a * DK, (a + 1) * DK)
                        last = act.copy(state_hi[rows, :, a, :], b_state[rows].rearrange(
                            "p (c n) -> p c n", c=2)[:, :, a * DV:(a + 1) * DV])
                    last.then_inc(state_high, 1)

            def gate(s, t, j):
                if not ffn_slot(s):
                    return
                u, f = (3 * t + j) % 2, s - FFN_LAG
                act.wait_ge(ffn_done[j], f + 1)
                if j == 2:
                    act.wait_ge(h_ready[0], f + 1)
                elif exists(f - 1):
                    act.wait_ge(h_ready[j + 1], f)
                act.activation(act_g[:, u], b_ffn[u][:, 0:256], ACT.Silu, scale=SCALE).then_inc(silu_done[j], 1)

            def split_h(s, t, j):
                if not ffn_slot(s):
                    return
                hb, u, f = 3 * (t % 2) + j, (3 * t + j) % 2, s - FFN_LAG
                act.wait_ge(h_ready[j], f + 1)
                if exists(f - 4):
                    act.wait_ge(down_done, f - 2 if t % 2 == 0 else f - 3)
                act.copy(h_hi[:, ((t - FFN_LAG) // 2) % 2, hb], h_full[:, u]).then_inc(h_high[j], 1)

            def split_ffn(c):
                act.wait_ge(wf_in[c], 16)
                act.copy(wf_hi[:, ffn_part(c)], wf_int[:, ffn_part(c)]).then_inc(wf_high, 1)

            def sum_low_ffn(c):
                act.wait_ge(wf_split, c + 1)
                act.activation(wf_int[:, ffn_part(c)].bitcast(F32), wf_lo[:, ffn_part(c)].bitcast(F32), ACT.Square,
                               accum_out=wide_rows[:, c:c + 1]).then_inc(low_squared, 1)

            act.wait_ge(filled, 1)
            act.activation(silu_first[:], half_neg[:, 0:1], ACT.Silu)
            split_xT(0, 0, 0)
            split_xT(1, 0, 1)
            for c in range(3):
                for k in range(KD):
                    act.wait_ge(wp_in[KD * c + k], 16)
                    act.copy(wp_hi[:, c, k], wp_raw[:, c, k]).then_inc(wp_high, 1)

            def slot(s, q, t, ahead):
                if not is_slot(s, NT):
                    split_qk(s, q, t)
                if sparse(s - 1):
                    split_kv(s - 1, *back(q, t, 1))
                gate(s - 1, t - 1, 2)
                if ahead:
                    split_xT(s + 2, *back(q, t, -2))
                keep_x1(s, q, t)
                copy_v(s, q, t)
                if is_slot(s, 1) or is_slot(s, 2) or is_slot(s, 3):
                    split_ffn((0, 1, 4)[s - 1])
                split_h(s - 1, t - 1, 2)
                split_x1T(s, q, t)
                if is_slot(s, FFN_LAG):
                    sum_low_ffn(4)
                    sum_low_ffn(5)
                gate_v(s, q, t)
                if is_slot(s, 2) or is_slot(s, 3):
                    split_ffn(2 if s == 2 else 5)
                split_y(s, q, t)
                mean_squares(s, q, t)
                split_state(s, q, t)
                if is_slot(s, 2):
                    split_ffn(3)
                    sum_low_ffn(0)
                if is_slot(s, 3):
                    for c in range(1, 4):
                        sum_low_ffn(c)
                gate(s, t, 0)
                if is_slot(s, NT - 1):
                    split_qk(NT, NSEQ, 0, lambda: split_h(s, t, 0))
                    gate(s, t, 1)
                else:
                    gate(s, t, 1)
                    split_h(s, t, 0)
                split_h(s, t, 1)
                if is_slot(s, NT - 1):
                    split_y(NT, NSEQ, 0)
                if not sparse(s):
                    split_kv(s, q, t)

            def drain():
                at = lambda t: (NT + t, NSEQ, t)
                mean_squares(*at(0))
                gate(NT - 1, -1, 2)
                split_x1T(*at(0))
                keep_x1(*at(0))
                split_h(NT - 1, -1, 2)
                split_y(*at(1))
                gate(NT, 0, 0)
                split_h(NT, 0, 0)
                gate(NT, 0, 1)
                split_h(NT, 0, 1)
                keep_x1(*at(1))
                gate(NT, 0, 2)
                split_h(NT, 0, 2)
                gate(NT + 1, 1, 0)
                split_x1T(*at(1))
                split_h(NT + 1, 1, 0)
                keep_x1(*at(2))
                gate(NT + 1, 1, 1)
                split_x1T(*at(2))
                split_h(NT + 1, 1, 1)
                gate(NT + 1, 1, 2)
                split_h(NT + 1, 1, 2)
                for t in (2, 3):
                    for j in range(3):
                        gate(NT + t, t, j)
                        split_h(NT + t, t, j)
                    keep_x1(*at(t + 1))

            walk_and_drain(act, slot, drain)

        @block.vector
        def _(dve):
            def split_w_proj(c, k, signal):
                dve.wait_ge(wp_high, KD * c + k + 1)
                dve.tensor_tensor(wp_lo[:, c, k], wp_raw[:, c, k], wp_hi[:, c, k].bitcast(F32),
                                  ALU.subtract).then_inc(signal, 1)

            def halves(ap):
                return ap.rearrange("p (c e f) -> p c e f", e=2, f=DK // 2)

            def split_ffn(c):
                part = ffn_part(c)
                dve.wait_ge(wf_high, c + 1)
                dve.tensor_tensor(wf_lo[:, part], wf_int[:, part], wf_hi[:, part].bitcast(F32),
                                  ALU.subtract).then_inc(wf_split, 1)

            def split_wo():
                dve.wait_ge(wo_scaled, 1)
                dve.tensor_copy(wo_hi[:], wo_raw[:]).then_inc(wo_high, 1)
                dve.wait_ge(wo_high, 1)
                dve.tensor_tensor(wo_lo[:], wo_raw[:], wo_hi[:].bitcast(F32), ALU.subtract).then_inc(wo_split, 1)

            def tell_wide():
                dve.wait_ge(wide_summed, 1)
                dve.tensor_scalar(wide_rows[:], b_ffn[0][:, 0:NFP], 0.0, None, ALU.not_equal, ALU.add,
                                  accum_out=wide_parts[:]).then_inc(wide_known, 1)
                dve.wait_ge(wide_known, 1)
                dve.tensor_copy(wide_flag[:], wide_parts[:]).then_inc(wide_known, 1)

            def split_qk(s, q, t):
                n, n7 = s - 1, s - DOWN_LAG - 1
                if exists(n):
                    dve.wait_ge(qkT_high, n + 1)
                    if exists(n7) and not is_slot(s, NT):
                        dve.wait_ge(z2_stats, n7 + 1)
                    dve.tensor_tensor(qkT_lo[:], b_turn[:].rearrange("p (b n) -> p b n", b=4), qkT_hi[:].bitcast(F32),
                                      ALU.subtract).then_inc(qkT_split, 1)

            def moments_2(n, tn, waited=False):
                if exists(n):
                    if not waited:
                        dve.wait_ge(z2_stats, n + 1)
                    dve.bn_aggr(mv2[:, tn % 2], st2[:, tn % 2]).then_inc(z2_moments, 1)

            def rotate_parts(s, q, t):
                if exists(s):
                    dve.wait_ge(qk_done, s + 1)
                    if isinstance(s, int) and s < TS:
                        dve.wait_ge(rope_in[s], 16)
                    if exists(s - 1):
                        dve.wait_ge(rotated, s)
                    src = halves(row_bank(t, 0)[:])
                    cos, sin = rope_sb[:, t, 0], rope_sb[:, t, 1]
                    both = cos.unsqueeze(2).broadcast_to((P, 2 * H, 2, DK // 2))
                    dve.tensor_tensor(halves(rot_c[:]), src, both, ALU.mult)
                    for e in range(2):
                        last = dve.tensor_tensor(halves(rot_s[:])[:, :, e], src[:, :, 1 - e], sin, ALU.mult)
                    last.then_inc(rot_parts, 1)

            def rotate(s, q, t):
                if exists(s):
                    dve.wait_ge(rot_parts, s + 1)
                    if exists(s - 2):
                        dve.wait_ge(qkT_done, s - 1)
                        dve.wait_ge(kv_split, states_to(*back(q, t, 2)))
                    for e, sign in ((0, ALU.subtract), (1, ALU.add)):
                        last = dve.tensor_tensor(halves(qk[:, t % 2])[:, :, e], halves(rot_c[:])[:, :, e],
                                                 halves(rot_s[:])[:, :, e], sign)
                    last.then_inc(rotated, 1)

            def hidden(s, t, j):
                if not ffn_slot(s):
                    return
                u, f = (3 * t + j) % 2, s - FFN_LAG
                dve.wait_ge(silu_done[j], f + 1)
                if j == 2:
                    dve.wait_ge(h_split[0], f + 1)
                elif exists(f - 1):
                    dve.wait_ge(h_split[j + 1], f)
                dve.tensor_tensor(h_full[:, u], b_ffn[u][:, 256:512], act_g[:, u], ALU.mult).then_inc(h_ready[j], 1)

            def norm_1(s, q, t):
                n, tn = s - X1T_LAG, back(q, t, X1T_LAG)[1]
                if exists(n):
                    dve.wait_ge(z1_rstd, n + 1)
                    if exists(n - 4):
                        dve.wait_ge(x1_kept, n - 3)
                        dve.wait_ge(x1T_done, n - 3)
                    dve.tensor_scalar(x1[:, tn, :], z1[:], mv1[:, 0:1], rs1[:, 0:1], ALU.subtract,
                                      ALU.mult).then_inc(x1_ready, 1)

            def norm_2(s, q, t):
                n, (qn, tn) = s - DOWN_LAG - 1, back(q, t, DOWN_LAG + 1)
                r = tn % 2
                if exists(n):
                    dve.wait_ge(z2_rstd, n + 1)
                    if exists(n - 2):
                        dve.wait_ge(stored[r], 16 * (2 * qn + tn // 2))
                    dve.tensor_scalar(x2[:, r, :], z2[:, r, :], mv2[:, r, 0:1], rs2[:, r, 0:1], ALU.subtract,
                                      ALU.mult).then_inc(x2_ready, 1)

            def mask(s, q, t):
                n = s - 1
                if exists(n):
                    dve.wait_ge(scores_done, n + 1)
                    if is_slot(s, 1):
                        dve.wait_ge(consts, 1)
                    if exists(n - 1):
                        dve.wait_ge(o_done, n)
                    dve.tensor_tensor(attn[:], b_score[:].rearrange("p (a b) -> p a b", a=H),
                                      causal[:].unsqueeze(1).broadcast_to((P, H, P)), ALU.mult).then_inc(masked, 1)

            def split_x1T(s, q, t):
                n = s - X1T_LAG
                if exists(n):
                    ring, at = ((t - 3) // 2) % 2, ((t - 3) % 2) * P
                    dve.wait_ge(x1T_high, n + 1)
                    dve.tensor_tensor(x1T_lo[:, ring, :, at:at + P],
                                      b_turn[:, 0:KD * P].rearrange("p (k n) -> p k n", k=KD),
                                      x1T_hi[:, ring, :, at:at + P].bitcast(F32), ALU.subtract).then_inc(x1T_split, 1)

            def split_y(s, q, t):
                n = s - 2
                if exists(n):
                    dve.wait_ge(yT_high, n + 1)
                    dve.tensor_tensor(yT_lo[:], b_turn[:], yT_hi[:].bitcast(F32), ALU.subtract).then_inc(yT_split, 1)

            def split_state(s, q, t):
                qn, tn = back(q, t, 1)
                if exists(s - 1) and tn < TS - 1:
                    dve.wait_ge(state_high, states_to(qn, tn))
                    for a in range(2):
                        rows = slice(a * DK, (a + 1) * DK)
                        last = dve.tensor_tensor(state_lo[rows, :, a, :], b_state[rows].rearrange(
                            "p (c n) -> p c n", c=2)[:, :, a * DV:(a + 1) * DV],
                            state_hi[rows, :, a, :].bitcast(F32), ALU.subtract)
                    last.then_inc(state_split, 1)

            def gated_output(s, q, t):
                n, tn = s - 1, back(q, t, 1)[1]
                if exists(n):
                    dve.wait_ge(rms_ready, n + 1)
                    dve.wait_ge(g_gated, n + 1)
                    if exists(n - 1):
                        dve.wait_ge(yT_done, n)
                    for h in range(H):
                        cols = slice(h * DV, (h + 1) * DV)
                        last = dve.scalar_tensor_tensor(y[:, cols], b_o[:, cols], rms[:, tn % 2, h:h + 1],
                                                        g_sb[:, tn % 2, cols], ALU.mult, ALU.mult)
                    last.then_inc(y_ready, 1)

            def residual_1(s, q, t):
                n, (qn, tn) = s - 2, back(q, t, 2)
                if exists(n):
                    dve.wait_ge(wo_done, n + 1)
                    dve.wait_ge(x_in[tn // 2], 16 * (qn + 1))
                    if exists(n - 1):
                        dve.wait_ge(x1_ready, n)
                    dve.tensor_tensor(z1[:], row_bank(t, 3)[:, 0:D], x_sb[:, tn, :], ALU.add).then_inc(z1_ready, 1)
                    dve.wait_ge(z1_ready, n + 1)
                    dve.bn_stats(st1[:], z1[:]).then_inc(z1_stats, 1)

            def moments_1(n, waited=False):
                if exists(n):
                    if not waited:
                        dve.wait_ge(z1_stats, n + 1)
                    dve.bn_aggr(mv1[:], st1[:]).then_inc(z1_moments, 1)

            def residual_2(s, q, t):
                n, tn = s - DOWN_LAG, back(q, t, DOWN_LAG)[1]
                if exists(n):
                    dve.wait_ge(down_done, n + 1)
                    dve.wait_ge(x1_kept, n + 1)
                    if exists(n - 2):
                        dve.wait_ge(x2_ready, n - 1)
                    if exists(s - 2):
                        dve.wait_ge(z1_stats, s - 1)
                    dve.scalar_tensor_tensor(z2[:, tn % 2], row_bank(t, 4)[:, 0:D], SCALE * SCALE, x1_late[:, tn, :],
                                             ALU.mult, ALU.add).then_inc(z2_ready, 1)

            def stats_2(s, q, t):
                n, tn = s - DOWN_LAG, back(q, t, DOWN_LAG)[1]
                if exists(n):
                    dve.wait_ge(z2_ready, n + 1)
                    dve.bn_stats(st2[:, tn % 2], z2[:, tn % 2]).then_inc(z2_stats, 1)

            def early(s):
                return isinstance(s, int) and 1 <= s < FFN_LAG

            def residual_first(s):
                return is_slot(s, FFN_LAG) or is_slot(s, FFN_LAG + 1)

            dve.wait_ge(filled, 1)
            for diag in (qdiag_hi, qdiag_lo, state_hi, state_lo):
                last = dve.tensor_copy(diag[:], attn[:].rearrange("p (c a) n -> p c a n", c=2))
            last.then_inc(cleared, 1)
            for c in range(2):
                for k in range(KD):
                    split_w_proj(c, k, wp_split)

            def slot(s, q, t):
                n2, n6, (q7, t7) = s - 2, s - DOWN_LAG, back(q, t, DOWN_LAG + 1)
                split_qk(s, q, t)
                moments_2(n6 - 1, t7, waited=True)
                rotate_parts(s, q, t)
                if is_slot(s, 0):
                    split_w_proj(2, 1, wp_split_g[1])
                hidden(s - 1, t - 1, 2)
                norm_1(s, q, t)
                norm_2(s, q, t)
                if early(s - 1):
                    gated_output(s - 1, *back(q, t, 1))
                mask(s, q, t)
                rotate(s, q, t)
                if is_slot(s, 1):
                    split_ffn(0)
                    split_wo()
                if is_slot(s, 2):
                    split_ffn(1)
                split_x1T(s, q, t)
                if is_slot(s, 3):
                    split_ffn(3)
                    split_ffn(4)
                if is_slot(s, FFN_LAG):
                    tell_wide()
                split_y(s, q, t)
                if is_slot(s, 2):
                    split_ffn(2)
                if is_slot(s, 3):
                    split_ffn(5)
                if is_slot(s, NT - 1):
                    hidden(s, t, 0)
                    split_qk(NT, NSEQ, 0)
                    split_state(s, q, t)
                    gated_output(s, q, t)
                    residual_1(s, q, t)
                    hidden(s, t, 1)
                    mask(NT, NSEQ, 0)
                    split_y(NT, NSEQ, 0)
                else:
                    split_state(s, q, t)
                    hidden(s, t, 0)
                    hidden(s, t, 1)
                    if not early(s) and not residual_first(s):
                        gated_output(s, q, t)
                    residual_1(s, q, t)
                    if residual_first(s):
                        gated_output(s, q, t)
                residual_2(s, q, t)
                moments_1(n2, waited=exists(n6))
                stats_2(s, q, t)

            def drain():
                at = lambda t: (NT + t, NSEQ, t)

                def sum_2(t):
                    residual_2(*at(t))
                    stats_2(*at(t))
                    moments_2(NT + t - DOWN_LAG, back(NSEQ, t, DOWN_LAG)[1])

                moments_2(NT - DOWN_LAG - 1, back(NSEQ, 0, DOWN_LAG + 1)[1])
                norm_1(*at(0))
                hidden(NT - 1, -1, 2)
                norm_2(*at(0))
                split_x1T(*at(0))
                gated_output(*at(0))
                residual_1(*at(0))
                moments_1(NT - 2)
                sum_2(0)
                split_y(*at(1))
                hidden(NT, 0, 0)
                hidden(NT, 0, 1)
                norm_1(*at(1))
                norm_2(*at(1))
                residual_1(*at(1))
                moments_1(NT - 1)
                hidden(NT, 0, 2)
                hidden(NT + 1, 1, 0)
                split_x1T(*at(1))
                norm_1(*at(2))
                sum_2(1)
                hidden(NT + 1, 1, 1)
                split_x1T(*at(2))
                hidden(NT + 1, 1, 2)
                norm_2(*at(2))
                hidden(NT + 2, 2, 0)
                sum_2(2)
                hidden(NT + 2, 2, 1)
                hidden(NT + 2, 2, 2)
                norm_2(*at(3))
                hidden(NT + 3, 3, 0)
                hidden(NT + 3, 3, 1)
                sum_2(3)
                hidden(NT + 3, 3, 2)
                norm_2(*at(4))
                sum_2(4)
                sum_2(5)
                norm_2(*at(5))
                norm_2(*at(6))

            walk_and_drain(dve, lambda s, q, t, ahead: slot(s, q, t), drain)

        @block.gpsimd
        def _(pool):
            pool.memset(ident[:], 0.0)
            pool.memset(ones[:], 1.0)
            pool.memset(causal[:], 1.0)
            pool.memset(attn[:], 0.0)
            pool.memset(eps[:], EPS)
            pool.memset(half_neg[:], -0.5).then_inc(filled, 1)
            pool.wait_ge(filled, 1)
            pool.affine_select(out=ident[:], in_=ident[:], compare_op=ALU.not_equal, fill=1.0, base=0,
                               pattern=[[-1, P]], channel_multiplier=1)
            pool.affine_select(out=causal[:], in_=causal[:], compare_op=ALU.is_ge, fill=0.0, base=0,
                               pattern=[[1, P]], channel_multiplier=-1).then_inc(consts, 1)

            def split_xT(s, q, t):
                ring, at = t // 2, (t % 2) * P
                pool.wait_ge(xT_high, s + 1)
                pool.tensor_tensor(xT_lo[:, ring, :, at:at + P], xT_raw[:, ring, :, at:at + P],
                                   xT_hi[:, ring, :, at:at + P].bitcast(F32), ALU.subtract).then_inc(xT_split, 1)

            def split_h(s, t, j):
                if not ffn_slot(s):
                    return
                u, hb = (3 * t + j) % 2, 3 * (t % 2) + j
                ring = ((t - FFN_LAG) // 2) % 2
                pool.wait_ge(h_high[j], s - FFN_LAG + 1)
                pool.tensor_tensor(h_lo[:, ring, hb], h_full[:, u], h_hi[:, ring, hb].bitcast(F32),
                                   ALU.subtract).then_inc(h_split[j], 1)

            def split_kv(s, q, t):
                if exists(s) and t < TS - 1:
                    pool.wait_ge(kv_high, states_to(q, t))
                    pool.tensor_tensor(k_lo[:], qk[:, t % 2, 256:512], k_hi[:].bitcast(F32), ALU.subtract)
                    pool.tensor_tensor(v_lo[:], v_sb[:, t % 2], v_hi[:].bitcast(F32), ALU.subtract).then_inc(kv_split, 1)

            def rms_norm(s, q, t):
                n, tn = s - 1, back(q, t, 1)[1]
                if exists(n):
                    pool.wait_ge(squared, 4 * n + 4)
                    if exists(n - 2):
                        pool.wait_ge(y_ready, n - 1)
                    pool.tensor_tensor(ms_eps[:, tn % 2], ms[:, tn % 2], eps[:], ALU.add).then_inc(ms_ready, 1)
                    pool.wait_ge(ms_ready, n + 1)
                    pool.tensor_tensor(rms[:, tn % 2], ms_eps[:, tn % 2], half_neg[:], ALU.pow).then_inc(rms_ready, 1)

            def inv_std(n, moments, var, rstd, mv, ve, rs):
                if exists(n):
                    pool.wait_ge(moments, n + 1)
                    pool.tensor_tensor(ve, mv[:, 1:2], eps[:, 0:1], ALU.add).then_inc(var, 1)
                    pool.wait_ge(var, n + 1)
                    pool.tensor_tensor(rs, ve, half_neg[:, 0:1], ALU.pow).then_inc(rstd, 1)

            def inv_std_1(s, q, t):
                inv_std(s - 2, z1_moments, z1_var, z1_rstd, mv1[:], ve1[:], rs1[:])

            def inv_std_2(s, q, t):
                r = back(q, t, DOWN_LAG + 1)[1] % 2
                inv_std(s - DOWN_LAG - 1, z2_moments, z2_var, z2_rstd, mv2[:, r], ve2[:, r], rs2[:, r])

            def scale_wo():
                pool.wait_ge(wo_in, 16)
                pool.wait_ge(gn_in, 16)
                flat = wo_raw[:].rearrange("p h n -> p (h n)")
                pool.tensor_tensor(flat, flat, gn_sb[:, 0:1].broadcast_to((P, H * D)), ALU.mult).then_inc(wo_scaled, 1)

            split_xT(0, 0, 0)
            split_xT(1, 0, 1)
            pool.wait_ge(wp_high, 2 * KD + 1)
            pool.tensor_tensor(wp_lo[:, 2, 0], wp_raw[:, 2, 0], wp_hi[:, 2, 0].bitcast(F32),
                               ALU.subtract).then_inc(wp_split_g[0], 1)

            def slot(s, q, t, ahead):
                inv_std_2(s, q, t)
                if sparse(s - 1):
                    split_kv(s - 1, *back(q, t, 1))
                if ahead:
                    split_xT(s + 2, *back(q, t, -2))
                if is_slot(s, 0):
                    scale_wo()
                split_h(s - 1, t - 1, 2)
                rms_norm(s, q, t)
                split_h(s, t, 0)
                split_h(s, t, 1)
                if not sparse(s):
                    split_kv(s, q, t)
                inv_std_1(s, q, t)

            def drain():
                at = lambda t: (NT + t, NSEQ, t)
                inv_std_2(*at(0))
                rms_norm(*at(0))
                split_h(NT - 1, -1, 2)
                inv_std_1(*at(0))
                inv_std_2(*at(1))
                split_h(NT, 0, 0)
                split_h(NT, 0, 1)
                inv_std_1(*at(1))
                split_h(NT, 0, 2)
                split_h(NT + 1, 1, 0)
                inv_std_2(*at(2))
                split_h(NT + 1, 1, 1)
                split_h(NT + 1, 1, 2)
                split_h(NT + 2, 2, 0)
                inv_std_2(*at(3))
                split_h(NT + 2, 2, 1)
                split_h(NT + 2, 2, 2)
                split_h(NT + 3, 3, 0)
                split_h(NT + 3, 3, 1)
                inv_std_2(*at(4))
                split_h(NT + 3, 3, 2)
                inv_std_2(*at(5))
                inv_std_2(*at(6))

            walk_and_drain(pool, slot, drain)


def kernel(L0_attn_x, L0_attn_Wq, L0_attn_Wk, L0_attn_Wv, L0_attn_Wg, L0_attn_Wo, L0_attn_gn_weight,
           L0_ffn_w_gate, L0_ffn_w_up, L0_ffn_w_down):
    import concourse.bacc as bacc
    from concourse.bass_utils import run_bass_kernel_spmd

    def laid(a):
        return np.ascontiguousarray(np.asarray(a))

    x = laid(L0_attn_x).reshape(-1, D)
    rows = lambda w: w.reshape(-1, P, w.shape[1]).transpose(1, 0, 2)
    proj = np.concatenate([np.asarray(w) for w in (L0_attn_Wq, L0_attn_Wk, L0_attn_Wv, L0_attn_Wg)], 1)
    gate_up = np.concatenate([np.asarray(L0_ffn_w_gate).T, np.asarray(L0_ffn_w_up).T], 1)
    arrays = {
        "in_xT": laid(rows(x.T)),
        "in_x": x,
        "in_w_proj": laid(rows(proj).reshape(P, KD, 3, 512).transpose(0, 2, 1, 3)),
        "in_w_o": laid(rows(np.asarray(L0_attn_Wo))),
        "in_gn": laid(L0_attn_gn_weight).reshape(P, 1),
        "in_w_ffn": np.concatenate([rows(gate_up).reshape(P, KD * 2 * HID),
                                    rows(np.asarray(L0_ffn_w_down).T).reshape(P, HB * D)], 1),
        "in_rope": rope_tables(),
    }
    nc = bacc.Bacc("TRN2", target_bir_lowering=False, num_devices=1)
    args = [nc.dram_tensor(n, a.shape, mybir.dt.from_np(a.dtype), kind="ExternalInput").ap()
            for n, a in arrays.items()]
    out = nc.dram_tensor("out_0", x.shape, F32, kind="ExternalOutput").ap()
    build_block(nc, *args, out)
    result = run_bass_kernel_spmd(nc, [arrays], core_ids=[0])
    return result.results[0]["out_0"].reshape(np.asarray(L0_attn_x).shape)
```
